# Optimizing a Trainium2 kernel written in Bass

```python
import numpy as np
import jax
import jax.numpy as jnp

def _softmax(x, axis=-1):
    return jax.nn.softmax(x, axis=axis)

def _gelu(x):
    return jax.nn.gelu(x, approximate=True)

def _silu(x):
    return jax.nn.silu(x)

def _sigmoid(x):
    return jax.nn.sigmoid(x)

def _layernorm(x, axis=-1, eps=1e-05):
    m = jnp.mean(x, axis=axis, keepdims=True)
    v = jnp.var(x, axis=axis, keepdims=True)
    return (x - m) / jnp.sqrt(v + eps)

def _scatter_add(tgt, idx, src, axis=0):
    return tgt.at[idx].add(src)

def _segment_sum(src, seg, n):
    return jax.ops.segment_sum(src, seg, n)
kernel_name = 'mk_seq_postln_d2_jaxref_r8_61ea13'

def setup_inputs(seed: int=0):
    np.random.seed(seed)
    _w = jnp.asarray

    def _L0_attn_setup():
        import jax, jax.numpy as jnp
        import numpy as np
        D_MODEL = 128
        N_HEADS = 16
        N_GROUPS = 4
        D_HEAD = D_MODEL // N_HEADS
        HPG = N_HEADS // N_GROUPS
        B, T = (2, 256)

        def _rope(x):
            t, d = (x.shape[2], x.shape[3])
            pos = jnp.arange(t, dtype=jnp.float32)[:, None]
            freq = jnp.exp(-(jnp.arange(0, d, 2, dtype=jnp.float32) / d) * jnp.log(jnp.float32(10000.0)))
            angle = pos * freq
            cos, sin = (jnp.cos(angle), jnp.sin(angle))
            xe, xo = (x[..., ::2], x[..., 1::2])
            re = xe * cos - xo * sin
            ro = xe * sin + xo * cos
            return jnp.stack([re, ro], axis=-1).reshape(x.shape)
        key = jax.random.key(seed)
        ks = jax.random.split(key, 10)
        s = 0.02
        return {'x': jax.random.normal(ks[0], (B, T, D_MODEL), dtype=jnp.float32), 'Wq': jax.random.normal(ks[1], (D_MODEL, D_MODEL), dtype=jnp.float32) * s, 'bq': jax.random.normal(ks[2], (D_MODEL,), dtype=jnp.float32) * s, 'Wk': jax.random.normal(ks[3], (D_MODEL, N_GROUPS * D_HEAD), dtype=jnp.float32) * s, 'bk': jax.random.normal(ks[4], (N_GROUPS * D_HEAD,), dtype=jnp.float32) * s, 'Wv': jax.random.normal(ks[5], (D_MODEL, N_GROUPS * D_HEAD), dtype=jnp.float32) * s, 'bv': jax.random.normal(ks[6], (N_GROUPS * D_HEAD,), dtype=jnp.float32) * s, 'Wo': jax.random.normal(ks[7], (D_MODEL, D_MODEL), dtype=jnp.float32) * s, 'bo': jax.random.normal(ks[8], (D_MODEL,), dtype=jnp.float32) * s}
    _L0_attn_in = _L0_attn_setup()

    def _L0_ffn_setup():
        import jax, jax.numpy as jnp
        import numpy as np
        N_EMBD = 128
        N_STATE = 512
        key = jax.random.key(seed)
        k_x, k_w1, k_b1, k_w2, k_b2 = jax.random.split(key, 5)
        x = jax.random.normal(k_x, (4, 256, N_EMBD), dtype=jnp.float32)
        w1 = jax.random.normal(k_w1, (N_EMBD, N_STATE), dtype=jnp.float32) * (1.0 / np.sqrt(N_EMBD))
        b1 = jax.random.normal(k_b1, (N_STATE,), dtype=jnp.float32) * 0.02
        w2 = jax.random.normal(k_w2, (N_STATE, N_EMBD), dtype=jnp.float32) * (1.0 / np.sqrt(N_STATE))
        b2 = jax.random.normal(k_b2, (N_EMBD,), dtype=jnp.float32) * 0.02
        return {'x': x, 'w1': w1, 'b1': b1, 'w2': w2, 'b2': b2}
    _L0_ffn_in = _L0_ffn_setup()

    def _L1_attn_setup():
        import jax, jax.numpy as jnp
        import numpy as np
        B, S, D_IN, D_OUT, H = (4, 256, 128, 128, 16)
        HD = D_OUT // H
        key = jax.random.key(seed)
        ks = jax.random.split(key, 6)
        scale_in = 1.0 / np.sqrt(D_IN)
        scale_out = 1.0 / np.sqrt(D_OUT)
        return {'x': jax.random.normal(ks[0], (B, S, D_IN), dtype=jnp.float32), 'Wq': jax.random.normal(ks[1], (D_IN, D_OUT), dtype=jnp.float32) * scale_in, 'Wk': jax.random.normal(ks[2], (D_IN, D_OUT), dtype=jnp.float32) * scale_in, 'Wv': jax.random.normal(ks[3], (D_IN, D_OUT), dtype=jnp.float32) * scale_in, 'Wo': jax.random.normal(ks[4], (D_OUT, D_OUT), dtype=jnp.float32) * scale_out, 'bo': jax.random.normal(ks[5], (D_OUT,), dtype=jnp.float32) * 0.01}
    _L1_attn_in = _L1_attn_setup()

    def _L1_ffn_setup():
        import jax, jax.numpy as jnp
        import numpy as np
        D_IN, D_HID = (128, 512)

        def _ternary(key, shape):
            return jax.random.randint(key, shape, -1, 2).astype(jnp.float32)

        def _tlin(x, w, s):
            return jnp.einsum('bsi,oi->bso', x, w) * s
        key = jax.random.key(seed)
        ks = jax.random.split(key, 12)
        inv = lambda fan: 1.0 / np.sqrt(fan).astype(np.float32)
        return {'x': jax.random.normal(ks[0], (4, 256, D_IN), dtype=jnp.float32), 'w1_w': _ternary(ks[1], (D_HID, D_IN)), 'w1_s': jax.random.uniform(ks[2], (D_HID,), dtype=jnp.float32) * inv(D_IN), 'w2_w': _ternary(ks[3], (D_HID, D_IN)), 'w2_s': jax.random.uniform(ks[4], (D_HID,), dtype=jnp.float32) * inv(D_IN), 'h1_w': _ternary(ks[5], (D_HID, D_HID)), 'h1_s': jax.random.uniform(ks[6], (D_HID,), dtype=jnp.float32) * inv(D_HID), 'h2_w': _ternary(ks[7], (D_HID, D_HID)), 'h2_s': jax.random.uniform(ks[8], (D_HID,), dtype=jnp.float32) * inv(D_HID), 'w3_w': _ternary(ks[9], (D_IN, D_HID)), 'w3_s': jax.random.uniform(ks[10], (D_IN,), dtype=jnp.float32) * inv(D_HID)}
    _L1_ffn_in = _L1_ffn_setup()
    _d = {'L0_attn_x': _L0_attn_in['x'], 'L0_attn_Wq': _L0_attn_in['Wq'], 'L0_attn_bq': _L0_attn_in['bq'], 'L0_attn_Wk': _L0_attn_in['Wk'], 'L0_attn_bk': _L0_attn_in['bk'], 'L0_attn_Wv': _L0_attn_in['Wv'], 'L0_attn_bv': _L0_attn_in['bv'], 'L0_attn_Wo': _L0_attn_in['Wo'], 'L0_attn_bo': _L0_attn_in['bo'], 'L0_ffn_w1': _L0_ffn_in['w1'], 'L0_ffn_b1': _L0_ffn_in['b1'], 'L0_ffn_w2': _L0_ffn_in['w2'], 'L0_ffn_b2': _L0_ffn_in['b2'], 'L1_attn_Wq': _L1_attn_in['Wq'], 'L1_attn_Wk': _L1_attn_in['Wk'], 'L1_attn_Wv': _L1_attn_in['Wv'], 'L1_attn_Wo': _L1_attn_in['Wo'], 'L1_attn_bo': _L1_attn_in['bo'], 'L1_ffn_w1_w': _L1_ffn_in['w1_w'], 'L1_ffn_w1_s': _L1_ffn_in['w1_s'], 'L1_ffn_w2_w': _L1_ffn_in['w2_w'], 'L1_ffn_w2_s': _L1_ffn_in['w2_s'], 'L1_ffn_h1_w': _L1_ffn_in['h1_w'], 'L1_ffn_h1_s': _L1_ffn_in['h1_s'], 'L1_ffn_h2_w': _L1_ffn_in['h2_w'], 'L1_ffn_h2_s': _L1_ffn_in['h2_s'], 'L1_ffn_w3_w': _L1_ffn_in['w3_w'], 'L1_ffn_w3_s': _L1_ffn_in['w3_s']}
    _x0 = _d['L0_attn_x']
    _d['L0_attn_x'] = jax.random.normal(jax.random.fold_in(jax.random.key(seed), 1), (1, 2048, 128), dtype=_x0.dtype)
    del _x0
    return _d

def reference(L0_attn_x, L0_attn_Wq, L0_attn_bq, L0_attn_Wk, L0_attn_bk, L0_attn_Wv, L0_attn_bv, L0_attn_Wo, L0_attn_bo, L0_ffn_w1, L0_ffn_b1, L0_ffn_w2, L0_ffn_b2, L1_attn_Wq, L1_attn_Wk, L1_attn_Wv, L1_attn_Wo, L1_attn_bo, L1_ffn_w1_w, L1_ffn_w1_s, L1_ffn_w2_w, L1_ffn_w2_s, L1_ffn_h1_w, L1_ffn_h1_s, L1_ffn_h2_w, L1_ffn_h2_s, L1_ffn_w3_w, L1_ffn_w3_s):

    def _L0_attn_ref(x, Wq, bq, Wk, bk, Wv, bv, Wo, bo):
        import jax, jax.numpy as jnp
        import numpy as np
        D_MODEL = 128
        N_HEADS = 16
        N_GROUPS = 4
        D_HEAD = D_MODEL // N_HEADS
        HPG = N_HEADS // N_GROUPS
        B, T = (2, 256)

        def _rope(x):
            t, d = (x.shape[2], x.shape[3])
            pos = jnp.arange(t, dtype=jnp.float32)[:, None]
            freq = jnp.exp(-(jnp.arange(0, d, 2, dtype=jnp.float32) / d) * jnp.log(jnp.float32(10000.0)))
            angle = pos * freq
            cos, sin = (jnp.cos(angle), jnp.sin(angle))
            xe, xo = (x[..., ::2], x[..., 1::2])
            re = xe * cos - xo * sin
            ro = xe * sin + xo * cos
            return jnp.stack([re, ro], axis=-1).reshape(x.shape)
        b, t, _ = x.shape
        q = (x @ Wq + bq).reshape(b, t, N_HEADS, D_HEAD).transpose(0, 2, 1, 3)
        k = (x @ Wk + bk).reshape(b, t, N_GROUPS, D_HEAD).transpose(0, 2, 1, 3)
        v = (x @ Wv + bv).reshape(b, t, N_GROUPS, D_HEAD).transpose(0, 2, 1, 3)
        k = jnp.repeat(k, HPG, axis=1)
        v = jnp.repeat(v, HPG, axis=1)
        q = _rope(q)
        k = _rope(k)
        scale = jnp.float32(np.sqrt(D_HEAD))
        scores = jnp.einsum('bhtd,bhsd->bhts', q, k) / scale
        causal = jnp.tril(jnp.ones((t, t), dtype=bool))
        scores = jnp.where(causal, scores, -jnp.inf)
        probs = jax.nn.softmax(scores, axis=-1)
        attn = jnp.einsum('bhts,bhsd->bhtd', probs, v)
        out = attn.transpose(0, 2, 1, 3).reshape(b, t, N_HEADS * D_HEAD)
        return out @ Wo + bo

    def _L0_ffn_ref(x, w1, b1, w2, b2):
        import jax, jax.numpy as jnp
        import numpy as np
        N_EMBD = 128
        N_STATE = 512
        h = jax.nn.gelu(jnp.einsum('bse,eh->bsh', x, w1) + b1, approximate=False)
        return jnp.einsum('bsh,he->bse', h, w2) + b2

    def _L1_attn_ref(x, Wq, Wk, Wv, Wo, bo):
        import jax, jax.numpy as jnp
        import numpy as np
        B, S, D_IN, D_OUT, H = (4, 256, 128, 128, 16)
        HD = D_OUT // H
        b, s, _ = x.shape

        def split(t):
            return t.reshape(b, s, H, HD).transpose(0, 2, 1, 3)
        q = split(x @ Wq)
        k = split(x @ Wk)
        v = split(x @ Wv)
        scores = jnp.einsum('bhqd,bhkd->bhqk', q, k) / jnp.sqrt(jnp.float32(HD))
        causal = jnp.tril(jnp.ones((s, s), dtype=bool))
        scores = jnp.where(causal, scores, -jnp.inf)
        weights = jax.nn.softmax(scores, axis=-1)
        ctx = jnp.einsum('bhqk,bhkd->bhqd', weights, v)
        ctx = ctx.transpose(0, 2, 1, 3).reshape(b, s, D_OUT)
        return ctx @ Wo + bo

    def _L1_ffn_ref(x, w1_w, w1_s, w2_w, w2_s, h1_w, h1_s, h2_w, h2_s, w3_w, w3_s):
        import jax, jax.numpy as jnp
        import numpy as np
        D_IN, D_HID = (128, 512)

        def _ternary(key, shape):
            return jax.random.randint(key, shape, -1, 2).astype(jnp.float32)

        def _tlin(x, w, s):
            return jnp.einsum('bsi,oi->bso', x, w) * s
        h = jax.nn.silu(_tlin(x, w1_w, w1_s)) * _tlin(x, w2_w, w2_s)
        h = jax.nn.gelu(_tlin(h, h1_w, h1_s), approximate=False)
        h = jax.nn.gelu(_tlin(h, h2_w, h2_s), approximate=False)
        return _tlin(h, w3_w, w3_s)
    x = L0_attn_x
    x = _layernorm(x + _L0_attn_ref(x, L0_attn_Wq, L0_attn_bq, L0_attn_Wk, L0_attn_bk, L0_attn_Wv, L0_attn_bv, L0_attn_Wo, L0_attn_bo), axis=-1)
    x = _layernorm(x + _L0_ffn_ref(x, L0_ffn_w1, L0_ffn_b1, L0_ffn_w2, L0_ffn_b2), axis=-1)
    x = _layernorm(x + _L1_attn_ref(x, L1_attn_Wq, L1_attn_Wk, L1_attn_Wv, L1_attn_Wo, L1_attn_bo), axis=-1)
    x = _layernorm(x + _L1_ffn_ref(x, L1_ffn_w1_w, L1_ffn_w1_s, L1_ffn_w2_w, L1_ffn_w2_s, L1_ffn_h1_w, L1_ffn_h1_s, L1_ffn_h2_w, L1_ffn_h2_s, L1_ffn_w3_w, L1_ffn_w3_s), axis=-1)
    return x

_drawn_inputs = setup_inputs


def setup_inputs(seed=0):
    import zlib

    import numpy as np

    out = dict(_drawn_inputs(seed))
    spreads = {}
    factors = {'L0_attn_Wq': 8.0,
     'L0_attn_bq': 8.0,
     'L0_attn_Wk': 8.0,
     'L0_attn_bk': 8.0,
     'L0_attn_Wv': 8.0,
     'L0_attn_bv': 8.0,
     'L0_attn_Wo': 5.986,
     'L0_ffn_b1': 4.568,
     'L1_attn_bo': 5.046,
     'L1_ffn_w1_w': 8.0,
     'L1_ffn_w1_s': 8.0,
     'L1_ffn_w2_w': 8.0,
     'L1_ffn_w2_s': 8.0,
     'L1_ffn_h1_w': 8.0,
     'L1_ffn_h1_s': 8.0,
     'L1_ffn_h2_w': 8.0,
     'L1_ffn_h2_s': 8.0,
     'L1_ffn_w3_w': 8.0,
     'L1_ffn_w3_s': 8.0}
    for name, (base, spread) in spreads.items():
        noise = np.random.default_rng([zlib.crc32(name.encode()), seed]).standard_normal(out[name].shape)
        drawn = base * np.exp(spread * noise) if base else spread * noise
        out[name] = jnp.asarray(drawn.astype(out[name].dtype))
    for name, factor in factors.items():
        out[name] = (out[name] * factor).astype(out[name].dtype)
    return out
```

```python
from contextlib import ExitStack

import concourse.bass as bass
from concourse import mybir

F32 = mybir.dt.float32
BF16 = mybir.dt.bfloat16
ALU = mybir.AluOpType
ACT = mybir.ActivationFunctionType
AX_X = mybir.AxisListType.X

T = 2048
D = 128
H = 16
HD = D // H
P = 128
CH = 512
NC = T // CH
TPC = CH // P
NT = T // P
QUADS = H // 4
HID = 512
KH = HID // P
ROWS = 64
MROW = 6 * HD
Q_PARTS = (0, 0, 1, 0, 2, 1)
K_PARTS = (0, 1, 0, 2, 0, 1)
SCALE = float(HD) ** -0.5
EPS = 1e-5

FIRST = ["Wq", "Wqs", "Wk", "Wks", "Wv", "ident"]
FIRST_W = [D, D, D, D, D, P]
VEC = ["bq", "bqs", "bk", "bks"]
REST = ["mask_ts", "mask_st", "Wo", "W1", "W2", "Wq1", "Wk1", "Wv1", "Wo1", "A", "B", "H1", "H2", "W3"]
REST_W = [P, P, D, HID, KH * D, D, D, D, D, HID, HID, KH * HID, KH * HID, KH * D]
COLS = ["b1", "sa", "sb", "s1", "s2"]


def offsets():
    at, off = 0, {}
    for n, w in list(zip(FIRST, FIRST_W)) + [(n, 1) for n in VEC]:
        off[n] = (at, w)
        at += w
    first = at
    for n, w in list(zip(REST, REST_W)) + [(n, KH) for n in COLS]:
        off[n] = (at, w)
        at += w
    return off, first, at


OFF, FIRST_END, PACK_W = offsets()
ROWV = ["bv", "bo", "b2", "bo1", "s3"]

def groups(c):
    full = [[(2 * k, 0, 0), (2 * k + 1, 0, CH)] for k in range(2 * c)]
    wide = [(4 * c, 0, 0), (4 * c + 1, P, CH), (4 * c + 3, 3 * P, CH + 3 * P)]
    narrow = [(4 * c + 2, 2 * P, 0)]
    return full + ([narrow, wide] if c else [wide, narrow])


GROUPS = [groups(c) for c in range(NC)]
STEPS = [len(g) for g in GROUPS]
STEP0 = [sum(STEPS[:c]) for c in range(NC)]
NSTEP = sum(STEPS)
MAXB = [4 * TPC * (c + 1) for c in range(NC)]
MAX0 = [sum(MAXB[:c]) for c in range(NC)]
NMAX = sum(MAXB)


def step_width(tiles):
    return max(col + CH - t0 for _, t0, col in tiles)


MLP1 = [("gate", 0), ("gate", 1), ("h1", 0), ("h1", 1), ("h2", 0), ("h2", 1), ("out", 0), ("gate", 2), ("out", 1),
        ("gate", 3), ("h1", 2), ("h1", 3), ("h2", 2), ("h2", 3), ("out", 2), ("out", 3)]


def mlp1_index(kind, c):
    before = MLP1[:MLP1.index((kind, c))]
    return KH * NC + KH * len([k for k, _ in before if k != "out"])


def program(nc, x_in, xT_in, pack, rows, cos, sin, out):
    with ExitStack() as ctx:
        def sb(name, shape, dt=F32):
            return ctx.enter_context(nc.sbuf_tensor(name, shape, dt))

        def psum(name, shape):
            return ctx.enter_context(nc.psum_tensor(name, shape, F32))

        def sem(name):
            return ctx.enter_context(nc.semaphore(name))

        q_all = nc.dram_tensor("q_all", (H, ROWS, T), BF16).ap()
        k_all = nc.dram_tensor("k_all", (H, ROWS, T), BF16).ap()
        q_quad = q_all.rearrange("(g a h) r t -> g (h r) a t", g=QUADS, a=2)
        k_quad = k_all.rearrange("(g a h) r t -> g (h r) a t", g=QUADS, a=2)

        W = sb("W", [P, PACK_W])
        R = sb("R", [P, len(ROWV), D])
        X = sb("X", [P, NT, D])
        XB = sb("XB", [P, NT, D])
        XT = sb("XT", [P, T])
        ident16 = sb("ident16", [P, P], BF16)
        mask_ts = sb("mask_ts", [P, P], BF16)
        mask_st = sb("mask_st", [P, P], BF16)
        fill = sb("fill", [P, 2, 2 * T], BF16)
        Qn = sb("Qn", [P, 2, CH], BF16)
        Kn = sb("Kn", [P, 2, 2, CH], BF16)
        Qr = sb("Qr", [P, 2, T], BF16)
        Kr = sb("Kr", [P, 2, 2, T], BF16)
        V = sb("V", [P, NT, H, HD])
        Vq = sb("Vq", [P, NT, 4, 32])
        work = sb("work", [P, 8 * 1024])
        probs = work[:, :].rearrange("p (s n) -> p s n", s=8)
        hid = work[:, :].rearrange("p (s k n) -> p s k n", s=4, k=KH)
        O = sb("O", [P, QUADS, T])
        flat = O[:, :, :].rearrange("p g t -> p (g t)")
        uq = flat[:, 0:CH]
        uk = flat[:, CH:2 * CH]
        tq = flat[:, 2 * CH:3 * CH]
        tk = flat[:, 3 * CH:4 * CH]
        rq = flat[:, 4 * CH:5 * CH]
        rk = flat[:, 5 * CH:6 * CH]
        angles = flat[:, 6 * CH:10 * CH].rearrange("p (s f n) -> p s f n", s=2, f=2)
        parts16 = flat[:, 10 * CH:16 * CH].bitcast(BF16).rearrange("p (s k n) -> p s k n", s=4, k=3)
        q_parts = [parts16[:, s] for s in (0, 1)]
        k_parts = [parts16[:, s] for s in (2, 3)]
        maxp = sb("maxp", [P, 2, 16, NC])
        mx = sb("mx", [P, 2, 16])
        mres = sb("mres", [P, 2, 16])
        nmax = sb("nmax", [P, 2, 16, 3], BF16)
        mrow = sb("mrow", [12, 2, CH], BF16)
        rden = sb("rden", [P, 2, H])
        attn = sb("attn", [P, 2, D])
        attnT = sb("attnT", [P, 2, D])
        Y = sb("Y", [P, 2, TPC, D])
        stats = sb("stats", [P, 2, TPC, 6])
        mean_var = sb("mean_var", [P, 2, TPC, 2])
        veps = sb("veps", [P, 2, TPC])
        rstd = sb("rstd", [P, 2, TPC])
        mhalf = sb("mhalf", [P, TPC])

        ST = psum("ST", [P, 2, 1024])
        MX = psum("MX", [P, 2, 512])
        OT = psum("OT", [P, 512])
        MT = psum("MT", [P, 512])
        half = [ST[:, b // 2, 512 * (b % 2):512 * (b % 2) + 512] for b in range(4)]

        def w(name, k=0, n=None):
            at, width = OFF[name]
            n = width if n is None else n
            return W[:, at + k * n:at + (k + 1) * n]

        def row(name):
            return R[:, ROWV.index(name), :]

        s_w1 = sem("s_w1")
        s_rest = sem("s_rest")
        s_rows = sem("s_rows")
        s_x = sem("s_x")
        s_ang = [sem("s_ang0"), sem("s_ang1")]
        s_cst = sem("s_cst")
        s_c16 = sem("s_c16")
        s_ones = sem("s_ones")
        s_proj = sem("s_proj")
        s_took = sem("s_took")
        s_rot = sem("s_rot")
        s_uq = sem("s_uq")
        s_uk = sem("s_uk")
        s_q1 = sem("s_q1")
        s_q2 = sem("s_q2")
        s_q3 = sem("s_q3")
        s_rq = sem("s_rq")
        s_k1 = sem("s_k1")
        s_k2 = sem("s_k2")
        s_k3 = sem("s_k3")
        s_rk = sem("s_rk")
        s_qst = [sem("s_qst0"), sem("s_qst1")]
        s_kst = [sem("s_kst0"), sem("s_kst1")]
        s_n = sem("s_n")
        s_kr = [sem(f"s_kr{k}") for k in range(NC)]
        s_qr = [sem(f"s_qr{k}") for k in range(NC)]
        s_vq = sem("s_vq")
        s_max = sem("s_max")
        s_red = sem("s_red")
        s_comb = sem("s_comb")
        s_nmax = sem("s_nmax")
        s_mtp = sem("s_mtp")
        s_mrow = sem("s_mrow")
        s_mq = [sem("s_mq0"), sem("s_mq1")]
        s_st = sem("s_st")
        s_exp = sem("s_exp")
        s_pv = sem("s_pv")
        s_oe = sem("s_oe")
        s_turn = sem("s_turn")
        s_rden = sem("s_rden")
        s_attn = sem("s_attn")
        s_atp = sem("s_atp")
        s_ate = sem("s_ate")
        s_wo = sem("s_wo")
        s_y = sem("s_y")
        s_yr = sem("s_yr")
        s_t3 = sem("s_t3")
        s_bn = sem("s_bn")
        s_mv = sem("s_mv")
        s_ve = sem("s_ve")
        s_rs = sem("s_rs")
        s_ln = sem("s_ln")
        s_xb = sem("s_xb")
        s_xtp = sem("s_xtp")
        s_xt = sem("s_xt")
        s_ha = sem("s_ha")
        s_hr = sem("s_hr")
        s_hb = sem("s_hb")
        s_hm = sem("s_hm")
        s_out = sem("s_out")

        block = ctx.enter_context(nc.Block())

        def q_src(c):
            return (Qn, 0) if c == 0 else (Qr, c * CH)

        @block.sync
        def _(sp):
            sp.dma_start(W[:, 0:FIRST_END], pack[:, 0:FIRST_END]).then_inc(s_w1, 16)
            sp.dma_start(XT[:, :], xT_in).then_inc(s_w1, 16)
            sp.dma_start(X[:, :, :], x_in[0].rearrange("(n p) d -> p n d", p=P)).then_inc(s_x, 16)
            sp.dma_start(W[:, FIRST_END:], pack[:, FIRST_END:]).then_inc(s_rest, 16)
            sp.wait_ge(s_cst, 2)
            for f, dst in enumerate((q_all, k_all)):
                sp.dma_start(dst[:, MROW:ROWS, :], fill[:, f, :]).then_inc(s_ones, 16)

            def store_parts(L):
                for c in range(NC):
                    n = NC * L + c
                    for done, parts, which, dst, landed in ((s_q3, q_parts, Q_PARTS, q_all, s_qst),
                                                            (s_k3, k_parts, K_PARTS, k_all, s_kst)):
                        sp.wait_ge(done, n + 1)
                        for term, part in enumerate(which):
                            sp.dma_start(dst[:, HD * term:HD * (term + 1), c * CH:(c + 1) * CH],
                                         parts[n % 2][:, part, :]).then_inc(landed[n % 2], 16)

            def load_first(g):
                sp.dma_start(Qn[:, :, :], q_quad[bass.ds(g, 1), :, :, 0:CH].rearrange("g p a t -> (g p) a t"))\
                  .then_inc(s_n, 16)
                load_keys(Kn, g, 0, s_n)

            def load_keys(K, g, k, landed):
                for h in range(2):
                    p0 = ROWS * h
                    sp.dma_start(K[p0:p0 + ROWS, :, h, k * CH:(k + 1) * CH],
                                 k_quad[bass.ds(g, 1), p0:p0 + ROWS, :, k * CH:(k + 1) * CH]
                                 .rearrange("g p a t -> (g p) a t")).then_inc(landed, 16)

            def load_queries(g, k):
                sp.dma_start(Qr[:, :, k * CH:(k + 1) * CH],
                             q_quad[bass.ds(g, 1), :, :, k * CH:(k + 1) * CH].rearrange("g p a t -> (g p) a t"))\
                  .then_inc(s_qr[k], 16)

            def place_max(L, g, c):
                G = QUADS * L + g
                sp.wait_ge(s_mrow, NC * G + c + 1)
                dst, at = q_src(c)
                for j in range(4):
                    p0 = ROWS * (j % 2) + MROW
                    sp.dma_start(dst[p0:p0 + 3, j // 2, at:at + CH], mrow[3 * j:3 * j + 3, c % 2, :])\
                      .then_inc(s_mq[c % 2], 16)

            def quad(L, g, last):
                G = QUADS * L + g
                place_max(L, g, 1)
                if not last:
                    sp.wait_ge(s_st, 4 * (NSTEP * G + STEP0[1]))
                    load_first(g + 1)
                place_max(L, g, 2)
                if not last:
                    sp.wait_ge(s_st, 4 * (NSTEP * G + STEP0[2]))
                    load_queries(g + 1, 1)
                place_max(L, g, 3)
                if not last:
                    sp.wait_ge(s_st, 4 * (NSTEP * G + STEP0[3]))
                    load_queries(g + 1, 2)
                    for k in range(2):
                        sp.wait_ge(s_st, 4 * (NSTEP * G + STEP0[3] + 2 * k + 2))
                        load_keys(Kr, g + 1, k, s_kr[k])
                    place_max(L, g + 1, 0)
                    for k in range(2, NC):
                        sp.wait_ge(s_st, 4 * (NSTEP * G + STEP0[3] + 2 * k + 2))
                        load_keys(Kr, g + 1, k, s_kr[k])
                    load_queries(g + 1, 3)

            for L in range(2):
                store_parts(L)
                if L == 0:
                    sp.wait_ge(s_ones, 32)
                for landed in s_qst + s_kst:
                    sp.wait_ge(landed, 16 * 6 * 2 * (L + 1))
                load_first(0)
                for k in range(NC):
                    load_keys(Kr, 0, k, s_kr[k])
                    if k:
                        load_queries(0, k)
                place_max(L, 0, 0)
                with sp.Fori(0, QUADS - 1) as g:
                    quad(L, g, False)
                quad(L, QUADS - 1, True)
            o_view = out[0].rearrange("(n p) d -> p n d", p=P)
            for c in range(NC):
                sp.wait_ge(s_ln, 3 * NC + c + 1)
                sp.dma_start(o_view[:, TPC * c:TPC * (c + 1), :], X[:, TPC * c:TPC * (c + 1), :]).then_inc(s_out, 16)
            sp.wait_ge(s_out, 16 * NC)

        @block.gpsimd
        def _(pool):
            pool.memset(fill[:, 0, :], 0.0).then_inc(s_cst, 1)
            pool.memset(fill[:, 1, :], 1.0).then_inc(s_cst, 1)
            pool.memset(mhalf[:, :], -0.5).then_inc(s_cst, 1)
            pool.memset(Vq[:, :, :, :], 0.0).then_inc(s_cst, 1)
            pool.wait_ge(s_cst, 4)
            pool.memset(Vq[:, :, :, HD:HD + 1], 1.0).then_inc(s_cst, 1)
            pool.dma_start(R[:, :, :].rearrange("p a b -> p (a b)"), rows.partition_broadcast(P)).then_inc(s_rows, 16)

            def add_bias(phase, name):
                for c in range(NC):
                    if phase:
                        pool.wait_ge(s_ln, NC * (phase - 1) + c + 1)
                    for i in range(TPC * c, TPC * (c + 1)):
                        ins = pool.tensor_tensor(XB[:, i, :], X[:, i, :], row(name), ALU.add)
                    ins.then_inc(s_xb, 1)

            def split_keys(L):
                for c in range(NC):
                    n = NC * L + c
                    pool.wait_ge(s_k1, n + 1)
                    pool.wait_ge(s_uk, n + 1)
                    pool.tensor_tensor(rk, uk, k_parts[n % 2][:, 0, :], ALU.subtract).then_inc(s_rk, 1)
                    pool.wait_ge(s_k2, n + 1)
                    pool.wait_ge(s_rk, n + 1)
                    pool.tensor_tensor(k_parts[n % 2][:, 2, :], rk, k_parts[n % 2][:, 1, :], ALU.subtract)\
                        .then_inc(s_k3, 1)

            def take_values(L, g, k):
                pool.tensor_copy(Vq[:, TPC * k:TPC * (k + 1), :, 0:HD],
                                 V[:, TPC * k:TPC * (k + 1), bass.ds(4 * g, 4), :]).then_inc(s_vq, 1)

            def attention(L):
                for k in range(NC):
                    pool.wait_ge(s_took, NC * L + k + 1)
                    take_values(L, 0, k)
                with pool.Fori(0, QUADS - 1) as g:
                    for k in range(NC):
                        pool.wait_ge(s_pv, NSTEP * (QUADS * L + g) + STEP0[3] + 2 * k + 2)
                        take_values(L, g + 1, k)

            def powers(phase):
                for c in range(NC):
                    n = NC * phase + c
                    pool.wait_ge(s_mv, n + 1)
                    pool.tensor_scalar(veps[:, n % 2, :], mean_var[:, n % 2, :, 1], EPS, None, ALU.add).then_inc(s_ve, 1)
                    pool.wait_ge(s_ve, n + 1)
                    pool.tensor_tensor(rstd[:, n % 2, :], veps[:, n % 2, :], mhalf[:, :], ALU.pow).then_inc(s_rs, 1)

            split_keys(0)
            pool.wait_ge(s_x, 16)
            pool.wait_ge(s_rows, 16)
            add_bias(0, "bo")
            attention(0)
            powers(0)
            add_bias(1, "b2")
            powers(1)
            add_bias(2, "bo1")
            split_keys(1)
            attention(1)
            powers(2)
            powers(3)

        @block.tensor
        def _(pe):
            def project(L):
                for c in range(NC):
                    n = NC * L + c
                    xt = XT[:, c * CH:(c + 1) * CH]
                    if L == 0:
                        if c == 0:
                            pe.wait_ge(s_w1, 32)
                    else:
                        pe.wait_ge(s_xt, NC + c + 1)
                    if c == 0 and L:
                        pe.wait_ge(s_hr, KH * NC)
                    if n:
                        pe.wait_ge(s_uq, n)
                    if L:
                        pe.matmul(half[0], w("Wq1"), xt, start=True, stop=True).then_inc(s_proj, 1)
                    else:
                        pe.matmul(half[0], w("Wq"), xt, start=True, stop=True)
                        pe.matmul(half[1], w("Wqs"), xt, start=True, stop=True).then_inc(s_proj, 1)
                    if n:
                        pe.wait_ge(s_uk, n)
                    if L:
                        pe.matmul(half[2], w("Wk1"), xt, start=True, stop=True).then_inc(s_proj, 1)
                    else:
                        pe.matmul(half[2], w("Wk"), xt, start=True, stop=True)
                        pe.matmul(half[3], w("Wks"), xt, start=True, stop=True).then_inc(s_proj, 1)
                    if n:
                        pe.wait_ge(s_took, n)
                    if L and c == 0:
                        pe.wait_ge(s_yr, 2 * NC)
                    for i in range(TPC):
                        mm = pe.matmul(MX[:, 0, i * P:(i + 1) * P], XT[:, c * CH + i * P:c * CH + (i + 1) * P],
                                       w("Wv1" if L else "Wv"), start=True, stop=True)
                    mm.then_inc(s_proj, 1)

            def max_block(L, g, c, b):
                n = NMAX * (QUADS * L + g) + MAX0[c] + b
                j, i, k = b % 4, (b // 4) % TPC, b // (4 * TPC)
                Q, at = q_src(c)
                K = Kr if c else Kn
                if b == 0:
                    if c:
                        pe.wait_ge(s_qr[c], 16 * (QUADS * L + g + 1))
                        for kk in range(c + 1):
                            pe.wait_ge(s_kr[kk], 32 * (QUADS * L + g + 1))
                    else:
                        pe.wait_ge(s_n, 48 * (QUADS * L + g + 1))
                if not (c == 0 and b < 2 and L == 0 and isinstance(g, int) and g == 0):
                    pe.wait_ge(s_red, n - 1)
                diag = k == c
                width = (i + 1) * P if diag else CH
                mm = pe.matmul(MX[:, b % 2, 0:width], Q[:, j // 2, at + i * P:at + (i + 1) * P],
                               K[:, j // 2, j % 2, k * CH:k * CH + width], start=True, stop=not diag)
                if diag:
                    mm = pe.matmul(MX[:, b % 2, i * P:(i + 1) * P], ident16[:, :], mask_ts[:, :], start=False,
                                   stop=True)
                mm.then_inc(s_max, 1)

            def max_rows(L, g, c):
                n = NC * (QUADS * L + g) + c
                pe.wait_ge(s_nmax, n + 1)
                pe.wait_ge(s_mrow, n)
                for i in range(TPC):
                    mm = pe.matmul(MT[0:12, i * P:(i + 1) * P],
                                   nmax[:, c % 2, 4 * i:4 * i + 4, :].rearrange("p j k -> p (j k)"), ident16[:, :],
                                   start=True, stop=True)
                mm.then_inc(s_mtp, 1)

            def scores(L, g, c, s, j):
                u = STEP0[c] + s
                idx = 4 * (NSTEP * (QUADS * L + g) + u) + j
                Q, at = q_src(c)
                K = Kr if c else Kn
                if s == 0 and j == 0:
                    pe.wait_ge(s_mq[c % 2], 64 * (2 * (QUADS * L + g) + c // 2 + 1))
                if u or j >= 2:
                    pe.wait_ge(s_exp, idx - 1)
                for tile, t0, col in GROUPS[c][s]:
                    diag = tile >= TPC * c
                    dst = ST[:, j % 2, col:col + CH - t0]
                    mm = pe.matmul(dst, K[:, j // 2, j % 2, tile * P:(tile + 1) * P],
                                   Q[:, j // 2, at + t0:at + CH], start=True, stop=not diag)
                    if diag:
                        mm = pe.matmul(ST[:, j % 2, col:col + P], ident16[:, :], mask_st[:, :], start=False, stop=True)
                mm.then_inc(s_st, 1)

            def sums(L, g, c, s):
                G = QUADS * L + g
                u = STEP0[c] + s
                if s == 0:
                    if c:
                        pe.wait_ge(s_oe, NC * G + c)
                    pe.wait_ge(s_vq, NC * G + c + 1)
                pe.wait_ge(s_exp, 4 * (NSTEP * G + u + 1))
                for tile, t0, col in GROUPS[c][s]:
                    for j in range(4):
                        lastmm = pe.matmul(OT[32 * j:32 * j + 32, t0:CH], Vq[:, tile, j, :],
                                           probs[:, 4 * (u % 2) + j, col:col + CH - t0],
                                           start=(tile == 0), stop=(s == STEPS[c] - 1 and tile == GROUPS[c][s][-1][0]),
                                           skip_group_check=True)
                lastmm.then_inc(s_pv, 1)

            def quad(L, g, last):
                before = None
                for c in range(NC):
                    if c < NC - 1:
                        ahead = (g, c + 1)
                    else:
                        ahead = None if last else (g + 1, 0)
                    nb = MAXB[ahead[1]] if ahead else 0
                    lots = STEPS[c] - 1
                    done = 0
                    for s in range(STEPS[c]):
                        scores(L, g, c, s, 0)
                        scores(L, g, c, s, 1)
                        if before:
                            sums(L, *before)
                        if ahead and s == STEPS[c] - 1:
                            max_rows(L, *ahead)
                        upto = nb * (s + 1) // lots if s < lots else nb
                        mid = (done + upto) // 2
                        for b in range(done, mid):
                            max_block(L, *ahead, b)
                        scores(L, g, c, s, 2)
                        for b in range(mid, upto):
                            max_block(L, *ahead, b)
                        scores(L, g, c, s, 3)
                        done = upto
                        before = (g, c, s)
                sums(L, *before)
                pe.wait_ge(s_oe, NC * (QUADS * L + g + 1))

            def turned_sums(L):
                pe.wait_ge(s_exp, 4 * NSTEP * QUADS * (L + 1))
                pe.wait_ge(s_red, NMAX * QUADS * (L + 1))
                for step in range(NT + 2):
                    if step < NT:
                        n = NT * L + step
                        if n >= 2:
                            pe.wait_ge(s_attn, n - 1)
                        for g in range(QUADS):
                            mm = pe.transpose(half[n % 2][:, g * P:(g + 1) * P], O[:, g, step * P:(step + 1) * P],
                                              w("ident"))
                        mm.then_inc(s_turn, 1)
                    if 1 <= step <= NT:
                        n = NT * L + step - 1
                        pe.wait_ge(s_attn, n + 1)
                        if n >= 2:
                            pe.wait_ge(s_ate, n - 1)
                        pe.transpose(half[2 + n % 2][:, 0:P], attn[:, n % 2, :], w("ident")).then_inc(s_atp, 1)
                    if step >= 2:
                        tile = step - 2
                        n = NT * L + tile
                        c, i = divmod(tile, TPC)
                        ln = 2 * NC * L + c
                        pe.wait_ge(s_ate, n + 1)
                        if i == 0 and ln >= 2:
                            pe.wait_ge(s_yr, ln - 1)
                        pe.matmul(MX[:, c % 2, i * P:(i + 1) * P], attnT[:, n % 2, :], w("Wo1" if L else "Wo"),
                                  start=True, stop=True).then_inc(s_wo, 1)
                    if step >= 9 and (step - 9) % TPC == 0:
                        channels(2 * NC * L + (step - 9) // TPC)
                channels(2 * NC * L + NC - 1)

            def channels(ln):
                pe.wait_ge(s_ln, ln + 1)
                pe.wait_ge(s_xt, ln)
                if ln % NC == 0:
                    pe.wait_ge(s_mrow, NC * QUADS * (ln // (2 * NC) + 1))
                c = ln % NC
                for i in range(TPC):
                    mm = pe.transpose(MT[:, i * P:(i + 1) * P], X[:, TPC * c + i, :], w("ident"))
                mm.then_inc(s_xtp, 1)

            def out_product(ln, slot, weight):
                c = ln % NC
                pe.wait_ge(s_yr, ln - 1)
                for i in range(TPC):
                    for k in range(KH):
                        mm = pe.matmul(MX[:, c % 2, i * P:(i + 1) * P], hid[:, slot, k, i * P:(i + 1) * P],
                                       w(weight, k, D), start=(k == 0), stop=(k == KH - 1))
                mm.then_inc(s_y, 1)

            def mlp0():
                pe.wait_ge(s_ate, NT)
                for step in range(NC + 2):
                    if step < NC:
                        pe.wait_ge(s_xt, step + 1)
                        for m in range(KH):
                            n = KH * step + m
                            if n >= 2:
                                pe.wait_ge(s_hr, n - 1)
                            pe.matmul(half[n % 2], w("W1", m, P), XT[:, step * CH:(step + 1) * CH],
                                      start=True, stop=True).then_inc(s_ha, 1)
                    if 1 <= step <= NC:
                        pe.wait_ge(s_hr, KH * step)
                        out_product(NC + step - 1, step - 1, "W2")
                    if step >= 2:
                        channels(NC + step - 2)

            def mlp1():
                pe.wait_ge(s_ate, 2 * NT)
                for kind, c in MLP1:
                    if kind == "out":
                        pe.wait_ge(s_hr, mlp1_index("h2", c) + KH)
                        out_product(3 * NC + c, c % 2, "W3")
                        continue
                    at = mlp1_index(kind, c)
                    if kind == "gate":
                        pe.wait_ge(s_xt, 2 * NC + c + 1)
                    elif kind == "h1":
                        pe.wait_ge(s_hm, KH * (c + 1))
                    else:
                        pe.wait_ge(s_hr, mlp1_index("h1", c) + KH)
                    for m in range(KH):
                        n = at + m
                        pe.wait_ge(s_hr, n - 1)
                        if kind == "gate":
                            pe.matmul(half[n % 2], w("A", m, P), XT[:, c * CH:(c + 1) * CH], start=True, stop=True)\
                              .then_inc(s_ha, 1)
                            b = KH * c + m
                            if b >= 2:
                                pe.wait_ge(s_hm, b - 1)
                            pe.matmul(half[2 + b % 2], w("B", m, P), XT[:, c * CH:(c + 1) * CH], start=True, stop=True)\
                              .then_inc(s_hb, 1)
                        else:
                            slot = c % 2 if kind == "h1" else 2 + c % 2
                            weight = "H1" if kind == "h1" else "H2"
                            for k in range(KH):
                                mm = pe.matmul(half[n % 2], w(weight, k, HID)[:, m * P:(m + 1) * P], hid[:, slot, k, :],
                                               start=(k == 0), stop=(k == KH - 1))
                            mm.then_inc(s_ha, 1)

            for L in range(2):
                project(L)
                if L == 0:
                    pe.wait_ge(s_rest, 16)
                    pe.wait_ge(s_c16, 7)
                    pe.wait_ge(s_cst, 5)
                pe.wait_ge(s_uk, NC * (L + 1))
                pe.wait_ge(s_took, NC * (L + 1))
                for b in range(MAXB[0]):
                    max_block(L, 0, 0, b)
                max_rows(L, 0, 0)
                with pe.Fori(0, QUADS - 1) as g:
                    quad(L, g, False)
                quad(L, QUADS - 1, True)
                turned_sums(L)
                (mlp1 if L else mlp0)()

        @block.scalar
        def _(act):
            def split(L):
                for c in range(NC):
                    n = NC * L + c
                    for u, r, parts, ready, rest, one, two, landed, scale in (
                            (uq, rq, q_parts, s_uq, s_rq, s_q1, s_q2, s_qst, SCALE),
                            (uk, rk, k_parts, s_uk, s_rk, s_k1, s_k2, s_kst, 1.0)):
                        act.wait_ge(ready, n + 1)
                        if n >= 2:
                            act.wait_ge(landed[n % 2], 96 * (n // 2))
                        act.activation(parts[n % 2][:, 0, :], u, ACT.Copy, scale=scale).then_inc(one, 1)
                        act.wait_ge(rest, n + 1)
                        act.activation(parts[n % 2][:, 1, :], r, ACT.Copy).then_inc(two, 1)
                    if L == 0 and c + 2 < NC:
                        load_angles(c + 2)

            def keep_rows(L, g, c):
                n = NC * (QUADS * L + g) + c
                act.wait_ge(s_mtp, n + 1)
                act.activation(mrow[:, c % 2, :], MT[0:12, :], ACT.Copy).then_inc(s_mrow, 1)

            def keep_sums(L, g, c):
                act.wait_ge(s_pv, NSTEP * (QUADS * L + g) + STEP0[c] + STEPS[c])
                act.activation(O[:, bass.ds(g, 1), c * CH:(c + 1) * CH].rearrange("p g t -> p (g t)"), OT[:, :],
                               ACT.Copy).then_inc(s_oe, 1)

            def quad(L, g, last):
                G = QUADS * L + g
                for c in range(NC):
                    for s in range(STEPS[c]):
                        u = STEP0[c] + s
                        width = step_width(GROUPS[c][s])
                        for j in range(4):
                            if j == 2 and s == 0 and c:
                                keep_sums(L, g, c - 1)
                            if j == 2 and s == STEPS[c] - 1 and not (last and c == NC - 1):
                                keep_rows(L, *((g, c + 1) if c < NC - 1 else (g + 1, 0)))
                            idx = 4 * (NSTEP * G + u) + j
                            act.wait_ge(s_st, idx + 1)
                            if u >= 2:
                                act.wait_ge(s_pv, NSTEP * G + u - 1)
                            act.activation(probs[:, 4 * (u % 2) + j, 0:width], ST[:, j % 2, 0:width], ACT.Exp)\
                               .then_inc(s_exp, 1)
                keep_sums(L, g, NC - 1)

            def keep_channels(ln):
                act.wait_ge(s_xtp, ln + 1)
                c = ln % NC
                act.activation(XT[:, c * CH:(c + 1) * CH], MT[:, :], ACT.Copy).then_inc(s_xt, 1)

            def keep_attention(L):
                for tile in range(NT):
                    n = NT * L + tile
                    act.wait_ge(s_atp, n + 1)
                    if n >= 2:
                        act.wait_ge(s_wo, n - 1)
                    act.activation(attnT[:, n % 2, :], half[2 + n % 2][:, 0:P], ACT.Copy).then_inc(s_ate, 1)
                    if tile >= 8 and (tile - 8) % TPC == 0:
                        keep_channels(2 * NC * L + (tile - 8) // TPC)
                for c in (2, 3):
                    keep_channels(2 * NC * L + c)

            def mlp0():
                for step in range(NC + 2):
                    if step < NC:
                        for m in range(KH):
                            n = KH * step + m
                            act.wait_ge(s_ha, n + 1)
                            act.activation(hid[:, step, m, :], half[n % 2], ACT.Gelu,
                                           bias=w("b1", m, 1)).then_inc(s_hr, 1)
                    if step >= 2:
                        keep_channels(NC + step - 2)

            def mlp1():
                for kind, c in MLP1:
                    if kind == "out":
                        continue
                    at = mlp1_index(kind, c)
                    if kind == "gate" and c >= 2:
                        act.wait_ge(s_y, NC + c - 1)
                    for m in range(KH):
                        n = at + m
                        act.wait_ge(s_ha, n + 1)
                        if kind == "gate":
                            act.activation(hid[:, c % 2, m, :], half[n % 2], ACT.Silu,
                                           scale=w("sa", m, 1)).then_inc(s_hr, 1)
                        elif kind == "h1":
                            act.activation(hid[:, 2 + c % 2, m, :], half[n % 2], ACT.Gelu,
                                           scale=w("s1", m, 1)).then_inc(s_hr, 1)
                        else:
                            act.activation(hid[:, c % 2, m, :], half[n % 2], ACT.Gelu,
                                           scale=w("s2", m, 1)).then_inc(s_hr, 1)

            def load_angles(c):
                if c >= 2:
                    act.wait_ge(s_rot, 2 * (c - 2) + 2)
                for f, table in enumerate((cos, sin)):
                    act.dma_start(angles[:, c % 2, f, :], table[:, c * CH:(c + 1) * CH]).then_inc(s_ang[c % 2], 16)

            load_angles(0)
            load_angles(1)
            for L in range(2):
                split(L)
                keep_rows(L, 0, 0)
                with act.Fori(0, QUADS - 1) as g:
                    quad(L, g, False)
                quad(L, QUADS - 1, True)
                keep_attention(L)
                (mlp1 if L else mlp0)()

        @block.vector
        def _(dve):
            def project(L):
                for c in range(NC):
                    n = NC * L + c
                    if L == 0:
                        dve.wait_ge(s_ang[c % 2], 32 * (c // 2 + 1))
                    for qk, (u, t, r, ready, b) in enumerate(((uq, tq, rq, s_uq, "bq"), (uk, tk, rk, s_uk, "bk"))):
                        dve.wait_ge(s_proj, 3 * n + qk + 1)
                        if n:
                            dve.wait_ge(s_k3 if qk else s_q3, n)
                        if L == 0:
                            dve.scalar_tensor_tensor(u, half[2 * qk], w(b), angles[:, c % 2, 0, :], ALU.add, ALU.mult)
                            dve.scalar_tensor_tensor(t, half[2 * qk + 1], w(b + "s"), angles[:, c % 2, 1, :], ALU.add,
                                                     ALU.mult).then_inc(s_rot, 1)
                            dve.wait_ge(s_rot, 2 * n + qk + 1)
                            dve.tensor_tensor(u, u, t, ALU.add).then_inc(ready, 1)
                        else:
                            dve.tensor_copy(u, half[2 * qk]).then_inc(ready, 1)
                    dve.wait_ge(s_proj, 3 * n + 3)
                    dst = V[:, TPC * c:TPC * (c + 1), :, :].rearrange("p n h d -> p n (h d)")
                    src = MX[:, 0, :].rearrange("p (n e) -> p n e", n=TPC)
                    if L == 0:
                        dve.tensor_tensor(dst, src, row("bv").unsqueeze(1).to_broadcast([P, TPC, D]), ALU.add)\
                           .then_inc(s_took, 1)
                    else:
                        dve.tensor_copy(dst, src).then_inc(s_took, 1)
                    dve.wait_ge(s_q1, n + 1)
                    dve.wait_ge(s_uq, n + 1)
                    dve.scalar_tensor_tensor(rq, uq, SCALE, q_parts[n % 2][:, 0, :], ALU.mult, ALU.subtract)\
                       .then_inc(s_rq, 1)
                    dve.wait_ge(s_q2, n + 1)
                    dve.wait_ge(s_rq, n + 1)
                    dve.tensor_tensor(q_parts[n % 2][:, 2, :], rq, q_parts[n % 2][:, 1, :], ALU.subtract)\
                       .then_inc(s_q3, 1)

            def max_chunk(L, g, c):
                G = QUADS * L + g
                for b in range(MAXB[c]):
                    n = NMAX * G + MAX0[c] + b
                    j, i, k = b % 4, (b // 4) % TPC, b // (4 * TPC)
                    width = (i + 1) * P if k == c else CH
                    dve.wait_ge(s_max, n + 1)
                    dve.reduce_max(maxp[:, c % 2, 4 * i + j, k:k + 1], MX[:, b % 2, 0:width], AX_X).then_inc(s_red, 1)
                n = NC * G + c
                dve.wait_ge(s_red, NMAX * G + MAX0[c] + MAXB[c])
                dve.reduce_max(mx[:, c % 2, :], maxp[:, c % 2, :, 0:c + 1], AX_X).then_inc(s_comb, 1)
                dve.wait_ge(s_comb, 4 * n + 1)
                nm = nmax[:, c % 2, :, :]
                dve.tensor_scalar(nm[:, :, 0], mx[:, c % 2, :], -1.0, None, ALU.mult).then_inc(s_comb, 1)
                dve.wait_ge(s_comb, 4 * n + 2)
                dve.scalar_tensor_tensor(mres[:, c % 2, :], mx[:, c % 2, :], -1.0, nm[:, :, 0], ALU.mult, ALU.subtract)\
                   .then_inc(s_comb, 1)
                dve.wait_ge(s_comb, 4 * n + 3)
                dve.tensor_copy(nm[:, :, 1], mres[:, c % 2, :]).then_inc(s_comb, 1)
                dve.wait_ge(s_comb, 4 * n + 4)
                dve.tensor_tensor(nm[:, :, 2], mres[:, c % 2, :], nm[:, :, 1], ALU.subtract).then_inc(s_nmax, 1)

            def quad(L, g, last):
                for c in range(1, NC):
                    max_chunk(L, g, c)
                if not last:
                    max_chunk(L, g + 1, 0)

            def branch(ln, product_done, count):
                c = ln % NC
                y = Y[:, ln % 2, :, :]
                bank = MX[:, c % 2, :].rearrange("p (n e) -> p n e", n=TPC)
                dve.wait_ge(product_done, count)
                if ln < 3 * NC:
                    dve.wait_ge(s_xb, ln + 1)
                    dve.tensor_tensor(y, bank, XB[:, TPC * c:TPC * (c + 1), :], ALU.add).then_inc(s_yr, 1)
                else:
                    dve.tensor_tensor(y, bank, row("s3").unsqueeze(1).to_broadcast([P, TPC, D]), ALU.mult)\
                       .then_inc(s_t3, 1)
                    dve.wait_ge(s_t3, c + 1)
                    dve.tensor_tensor(y, y, X[:, TPC * c:TPC * (c + 1), :], ALU.add).then_inc(s_yr, 1)
                dve.wait_ge(s_yr, ln + 1)
                for i in range(TPC):
                    ins = dve.bn_stats(stats[:, ln % 2, i, :], Y[:, ln % 2, i, :])
                ins.then_inc(s_bn, 1)
                dve.wait_ge(s_bn, ln + 1)
                for i in range(TPC):
                    ins = dve.bn_aggr(mean_var[:, ln % 2, i, :], stats[:, ln % 2, i, :])
                ins.then_inc(s_mv, 1)

            def normalise(ln):
                c = ln % NC
                dve.wait_ge(s_rs, ln + 1)
                for i in range(TPC):
                    ins = dve.tensor_scalar(X[:, TPC * c + i, :], Y[:, ln % 2, i, :], mean_var[:, ln % 2, i, 0:1],
                                            rstd[:, ln % 2, i:i + 1], ALU.subtract, ALU.mult)
                ins.then_inc(s_ln, 1)

            def attention_out(L):
                for tile in range(NT):
                    n = NT * L + tile
                    dve.wait_ge(s_turn, n + 1)
                    bank = half[n % 2].rearrange("p (h e) -> p h e", h=H)
                    dve.reciprocal(rden[:, n % 2, :], bank[:, :, HD]).then_inc(s_rden, 1)
                    dve.wait_ge(s_rden, n + 1)
                    if n >= 2:
                        dve.wait_ge(s_atp, n - 1)
                    dve.tensor_tensor(attn[:, n % 2, :].rearrange("p (h e) -> p h e", h=H), bank[:, :, 0:HD],
                                      rden[:, n % 2, :].unsqueeze(2).to_broadcast([P, H, HD]), ALU.mult)\
                       .then_inc(s_attn, 1)
                    if tile >= 5 and (tile - 5) % TPC == 0:
                        c = (tile - 5) // TPC
                        branch(2 * NC * L + c, s_wo, NT * L + TPC * (c + 1))
                    if tile >= 7 and (tile - 7) % TPC == 0:
                        normalise(2 * NC * L + (tile - 7) // TPC)
                branch(2 * NC * L + 3, s_wo, NT * (L + 1))
                normalise(2 * NC * L + 3)

            def mlp0():
                for c in range(NC + 1):
                    if c < NC:
                        branch(NC + c, s_y, c + 1)
                    if c:
                        normalise(NC + c - 1)

            def mlp1():
                for kind, c in MLP1:
                    if kind == "gate":
                        for m in range(KH):
                            b = KH * c + m
                            dve.wait_ge(s_hb, b + 1)
                            dve.wait_ge(s_hr, mlp1_index("gate", c) + m + 1)
                            h = hid[:, c % 2, m, :]
                            dve.scalar_tensor_tensor(h, half[2 + b % 2], w("sb", m, 1), h, ALU.mult, ALU.mult)\
                               .then_inc(s_hm, 1)
                    if kind == "out":
                        branch(3 * NC + c, s_y, NC + c + 1)
                        normalise(3 * NC + c)

            for K in (Kn, Kr):
                for h in range(2):
                    dve.memset(K[ROWS * (1 - h):ROWS * (2 - h), :, h, :], 0.0).then_inc(s_c16, 1)
            dve.wait_ge(s_w1, 32)
            dve.tensor_copy(ident16[:, :], w("ident")).then_inc(s_c16, 1)
            dve.wait_ge(s_rows, 16)
            for L in range(2):
                project(L)
                if L == 0:
                    dve.wait_ge(s_rest, 16)
                    dve.tensor_copy(mask_ts[:, :], w("mask_ts")).then_inc(s_c16, 1)
                    dve.tensor_copy(mask_st[:, :], w("mask_st")).then_inc(s_c16, 1)
                max_chunk(L, 0, 0)
                with dve.Fori(0, QUADS - 1) as g:
                    quad(L, g, False)
                quad(L, QUADS - 1, True)
                attention_out(L)
                (mlp1 if L else mlp0)()


def kernel(**inputs):
    import numpy as np
    import concourse.bacc as bacc
    from concourse import mybir as mb
    from concourse.bass_utils import run_bass_kernel_spmd

    a = {k: np.ascontiguousarray(v) for k, v in inputs.items()}
    pair = np.arange(D) ^ 1
    spread = (np.arange(H) // 4)[:, None] * HD + np.arange(HD)[None]
    spread = spread.reshape(-1)

    def tiles(m):
        return m.reshape(-1, P, m.shape[1]).transpose(1, 0, 2).reshape(P, -1)

    def cols(v):
        return v.reshape(-1, P).T

    low = np.float32(-1e30)
    later = np.arange(P)[None, :] > np.arange(P)[:, None]
    freq = np.exp(-(np.arange(0, HD, 2, dtype=np.float32) / np.float32(HD)) * np.log(np.float32(10000.0)))
    angle = np.arange(T, dtype=np.float32)[None, :] * freq.astype(np.float32)[(np.arange(D) % HD) // 2][:, None]
    sign = np.where(np.arange(D) % 2 == 0, -1.0, 1.0)[:, None]
    cos = np.cos(angle.astype(np.float64)).astype(np.float32)
    sin = (np.sin(angle.astype(np.float64)) * sign).astype(np.float32)

    Wk, Wv = a["L0_attn_Wk"][:, spread], a["L0_attn_Wv"][:, spread]
    bk, bv = a["L0_attn_bk"][spread], a["L0_attn_bv"][spread]
    m = {
        "Wq": a["L0_attn_Wq"], "Wqs": a["L0_attn_Wq"][:, pair], "Wk": Wk, "Wks": Wk[:, pair], "Wv": Wv,
        "ident": np.eye(P, dtype=np.float32),
        "bq": cols(a["L0_attn_bq"]), "bqs": cols(a["L0_attn_bq"][pair]), "bk": cols(bk), "bks": cols(bk[pair]),
        "mask_ts": np.where(later, low, np.float32(0)), "mask_st": np.where(later.T, low, np.float32(0)),
        "Wo": a["L0_attn_Wo"], "W1": a["L0_ffn_w1"], "W2": tiles(a["L0_ffn_w2"]),
        "Wq1": a["L1_attn_Wq"], "Wk1": a["L1_attn_Wk"], "Wv1": a["L1_attn_Wv"], "Wo1": a["L1_attn_Wo"],
        "A": a["L1_ffn_w1_w"].T, "B": a["L1_ffn_w2_w"].T, "H1": tiles(a["L1_ffn_h1_w"].T),
        "H2": tiles(a["L1_ffn_h2_w"].T), "W3": tiles(a["L1_ffn_w3_w"].T),
        "b1": cols(a["L0_ffn_b1"]), "sa": cols(a["L1_ffn_w1_s"]), "sb": cols(a["L1_ffn_w2_s"]),
        "s1": cols(a["L1_ffn_h1_s"]), "s2": cols(a["L1_ffn_h2_s"]),
    }
    pack = np.zeros((P, PACK_W), np.float32)
    for name, (at, width) in OFF.items():
        pack[:, at:at + width] = m[name]
    rows = np.concatenate([bv, a["L0_attn_bo"], a["L0_ffn_b2"], a["L1_attn_bo"], a["L1_ffn_w3_s"]])[None, :]
    arrays = {"x_in": a["L0_attn_x"], "xT_in": np.ascontiguousarray(a["L0_attn_x"][0].T), "pack": pack, "rows": rows,
              "cos": cos, "sin": sin}
    nc = bacc.Bacc("TRN2", target_bir_lowering=False, num_devices=1)
    args = [nc.dram_tensor(k, v.shape, mb.dt.from_np(v.dtype), kind="ExternalInput").ap() for k, v in arrays.items()]
    args.append(nc.dram_tensor("y_out", (1, T, D), mb.dt.float32, kind="ExternalOutput").ap())
    program(nc, *args)
    r = run_bass_kernel_spmd(nc, [arrays], core_ids=[0])
    return r.results[0]["y_out"]
```

```python
from contextlib import ExitStack

import concourse.bass as bass
from concourse import mybir

F32 = mybir.dt.float32
BF16 = mybir.dt.bfloat16
ALU = mybir.AluOpType
ACT = mybir.ActivationFunctionType
AX_X = mybir.AxisListType.X

T = 2048
D = 128
H = 16
HD = D // H
P = 128
CH = 512
NC = T // CH
TPC = CH // P
NT = T // P
QUADS = H // 4
HID = 512
KH = HID // P
ROWS = 64
MROW = 6 * HD
Q_PARTS = (0, 0, 1, 0, 2, 1)
K_PARTS = (0, 1, 0, 2, 0, 1)
SCALE = float(HD) ** -0.5
EPS = 1e-5

FIRST = ["Wq", "Wqs", "Wk", "Wks", "Wv", "ident"]
FIRST_W = [D, D, D, D, D, P]
VEC = ["bq", "bqs", "bk", "bks"]
REST = ["mask_ts", "mask_st", "Wo", "W1", "W2", "Wq1", "Wk1", "Wv1", "Wo1", "A", "B", "H1", "H2", "W3"]
REST_W = [P, P, D, HID, KH * D, D, D, D, D, HID, HID, KH * HID, KH * HID, KH * D]
COLS = ["b1", "sa", "sb", "s1", "s2"]


def offsets():
    at, off = 0, {}
    for n, w in list(zip(FIRST, FIRST_W)) + [(n, 1) for n in VEC]:
        off[n] = (at, w)
        at += w
    first = at
    for n, w in list(zip(REST, REST_W)) + [(n, KH) for n in COLS]:
        off[n] = (at, w)
        at += w
    return off, first, at


OFF, FIRST_END, PACK_W = offsets()
ROWV = ["bv", "bo", "b2", "bo1", "s3"]

def groups(c):
    full = [[(2 * k, 0, 0), (2 * k + 1, 0, CH)] for k in range(2 * c)]
    wide = [(4 * c, 0, 0), (4 * c + 1, P, CH), (4 * c + 3, 3 * P, CH + 3 * P)]
    narrow = [(4 * c + 2, 2 * P, 0)]
    return full + ([narrow, wide] if c else [wide, narrow])


GROUPS = [groups(c) for c in range(NC)]
STEPS = [len(g) for g in GROUPS]
STEP0 = [sum(STEPS[:c]) for c in range(NC)]
NSTEP = sum(STEPS)
MAXB = [4 * TPC * (c + 1) for c in range(NC)]
MAX0 = [sum(MAXB[:c]) for c in range(NC)]
NMAX = sum(MAXB)


BLOCKS_BY = {0: 0, 5: MAXB[2], 11: MAXB[2] + MAXB[3], 13: MAXB[2] + MAXB[3], 16: MAXB[2] + MAXB[3] + MAXB[0], 19: NMAX,
             NSTEP: NMAX}
ROWS_AT = {5: (0, 2), 11: (0, 3), 16: (1, 0), 19: (1, 1)}
STREAM = [(0, 2, b) for b in range(MAXB[2])] + [(0, 3, b) for b in range(MAXB[3])] + \
         [(1, 0, b) for b in range(MAXB[0])] + [(1, 1, b) for b in range(MAXB[1])]


def step_width(tiles):
    return max(col + CH - t0 for _, t0, col in tiles)


MLP1 = [("gate", 0), ("gate", 1), ("h1", 0), ("h1", 1), ("h2", 0), ("h2", 1), ("out", 0), ("gate", 2), ("out", 1),
        ("gate", 3), ("h1", 2), ("h1", 3), ("h2", 2), ("h2", 3), ("out", 2), ("out", 3)]


def mlp1_index(kind, c):
    before = MLP1[:MLP1.index((kind, c))]
    return KH * NC + KH * len([k for k, _ in before if k != "out"])


def program(nc, x_in, xT_in, pack, rows, cos, sin, out):
    with ExitStack() as ctx:
        def sb(name, shape, dt=F32):
            return ctx.enter_context(nc.sbuf_tensor(name, shape, dt))

        def psum(name, shape):
            return ctx.enter_context(nc.psum_tensor(name, shape, F32))

        def sem(name):
            return ctx.enter_context(nc.semaphore(name))

        q_all = nc.dram_tensor("q_all", (H, ROWS, T), BF16).ap()
        k_all = nc.dram_tensor("k_all", (H, ROWS, T), BF16).ap()
        q_quad = q_all.rearrange("(g a h) r t -> g (h r) a t", g=QUADS, a=2)
        k_quad = k_all.rearrange("(g a h) r t -> g (h r) a t", g=QUADS, a=2)

        W = sb("W", [P, PACK_W])
        R = sb("R", [P, len(ROWV), D])
        X = sb("X", [P, NT, D])
        XB = sb("XB", [P, NT, D])
        XT = sb("XT", [P, T])
        ident16 = sb("ident16", [P, P], BF16)
        mask_ts = sb("mask_ts", [P, P], BF16)
        mask_st = sb("mask_st", [P, P], BF16)
        Qn = sb("Qn", [P, 2, 2 * CH], BF16)
        Kn = sb("Kn", [P, 2, 2, 2 * CH], BF16)
        Qr = sb("Qr", [P, 2, 2 * CH], BF16)
        Kr = sb("Kr", [P, 2, 2, T], BF16)
        V = sb("V", [P, NT, H, HD])
        Vq = sb("Vq", [P, NT, 4, 32])
        work = sb("work", [P, 8 * 1024])
        probs = work[:, :].rearrange("p (s n) -> p s n", s=8)
        hid = work[:, :].rearrange("p (s k n) -> p s k n", s=4, k=KH)
        O = sb("O", [P, QUADS, T])
        flat = O[:, :, :].rearrange("p g t -> p (g t)")
        uq = flat[:, 0:CH]
        uk = flat[:, CH:2 * CH]
        tq = flat[:, 2 * CH:3 * CH]
        tk = flat[:, 3 * CH:4 * CH]
        rq = flat[:, 4 * CH:5 * CH]
        rk = flat[:, 5 * CH:6 * CH]
        angles = flat[:, 6 * CH:10 * CH].rearrange("p (s f n) -> p s f n", s=2, f=2)
        parts16 = flat[:, 10 * CH:16 * CH].bitcast(BF16).rearrange("p (s k n) -> p s k n", s=4, k=3)
        q_parts = [parts16[:, s] for s in (0, 1)]
        k_parts = [parts16[:, s] for s in (2, 3)]
        fill = work[:, 0:2 * T].bitcast(BF16).rearrange("p (f n) -> p f n", f=2)
        maxp = sb("maxp", [P, 2, 16, NC])
        mx = sb("mx", [P, 2, 16])
        mres = sb("mres", [P, 2, 16])
        nmax = sb("nmax", [P, 2, 16, 3], BF16)
        mrow = sb("mrow", [12, 2, CH], BF16)
        rden = sb("rden", [P, 2, H])
        attn = sb("attn", [P, 2, D])
        attnT = sb("attnT", [P, 2, D])
        Y = sb("Y", [P, 2, TPC, D])
        stats = sb("stats", [P, 2, TPC, 6])
        mean_var = sb("mean_var", [P, 2, TPC, 2])
        veps = sb("veps", [P, 2, TPC])
        rstd = sb("rstd", [P, 2, TPC])
        mhalf = sb("mhalf", [P, TPC])

        ST = psum("ST", [P, 2, 1024])
        MX = psum("MX", [P, 2, 512])
        OT = psum("OT", [P, 512])
        MT = psum("MT", [P, 512])
        half = [ST[:, b // 2, 512 * (b % 2):512 * (b % 2) + 512] for b in range(4)]

        def w(name, k=0, n=None):
            at, width = OFF[name]
            n = width if n is None else n
            return W[:, at + k * n:at + (k + 1) * n]

        def row(name):
            return R[:, ROWV.index(name), :]

        s_w1 = sem("s_w1")
        s_rest = sem("s_rest")
        s_rows = sem("s_rows")
        s_x = sem("s_x")
        s_ang = [sem("s_ang0"), sem("s_ang1")]
        s_cst = sem("s_cst")
        s_c16 = sem("s_c16")
        s_ones = sem("s_ones")
        s_proj = sem("s_proj")
        s_took = sem("s_took")
        s_rot = sem("s_rot")
        s_uq = sem("s_uq")
        s_uk = sem("s_uk")
        s_q1 = sem("s_q1")
        s_q2 = sem("s_q2")
        s_q3 = sem("s_q3")
        s_rq = sem("s_rq")
        s_k1 = sem("s_k1")
        s_k2 = sem("s_k2")
        s_k3 = sem("s_k3")
        s_rk = sem("s_rk")
        s_qst = [sem("s_qst0"), sem("s_qst1")]
        s_kst = [sem("s_kst0"), sem("s_kst1")]
        s_n = [sem("s_n0"), sem("s_n1")]
        s_kr = [sem(f"s_kr{k}") for k in range(NC)]
        s_qr = [sem(f"s_qr{k}") for k in range(NC)]
        s_vq = sem("s_vq")
        s_max = sem("s_max")
        s_red = sem("s_red")
        s_comb = sem("s_comb")
        s_nmax = sem("s_nmax")
        s_mtp = sem("s_mtp")
        s_mrow = sem("s_mrow")
        s_mq = [sem("s_mq0"), sem("s_mq1")]
        s_st = sem("s_st")
        s_exp = sem("s_exp")
        s_pv = sem("s_pv")
        s_oe = sem("s_oe")
        s_turn = sem("s_turn")
        s_rden = sem("s_rden")
        s_attn = sem("s_attn")
        s_atp = sem("s_atp")
        s_ate = sem("s_ate")
        s_wo = sem("s_wo")
        s_y = sem("s_y")
        s_yr = sem("s_yr")
        s_t3 = sem("s_t3")
        s_bn = sem("s_bn")
        s_mv = sem("s_mv")
        s_ve = sem("s_ve")
        s_rs = sem("s_rs")
        s_ln = sem("s_ln")
        s_xb = sem("s_xb")
        s_xtp = sem("s_xtp")
        s_xt = sem("s_xt")
        s_ha = sem("s_ha")
        s_hr = sem("s_hr")
        s_hb = sem("s_hb")
        s_hm = sem("s_hm")
        s_out = sem("s_out")

        block = ctx.enter_context(nc.Block())

        def q_src(c):
            return (Qn, c * CH) if c < 2 else (Qr, (c - 2) * CH)

        @block.sync
        def _(sp):
            sp.dma_start(W[:, 0:FIRST_END], pack[:, 0:FIRST_END]).then_inc(s_w1, 16)
            sp.dma_start(XT[:, :], xT_in).then_inc(s_w1, 16)
            sp.dma_start(X[:, :, :], x_in[0].rearrange("(n p) d -> p n d", p=P)).then_inc(s_x, 16)
            sp.dma_start(W[:, FIRST_END:], pack[:, FIRST_END:]).then_inc(s_rest, 16)
            sp.wait_ge(s_cst, 2)
            for f, dst in enumerate((q_all, k_all)):
                sp.dma_start(dst[:, MROW:ROWS, :], fill[:, f, :]).then_inc(s_ones, 16)

            def store_parts(L):
                for c in range(NC):
                    n = NC * L + c
                    for done, parts, which, dst, landed in ((s_q3, q_parts, Q_PARTS, q_all, s_qst),
                                                            (s_k3, k_parts, K_PARTS, k_all, s_kst)):
                        sp.wait_ge(done, n + 1)
                        for term, part in enumerate(which):
                            sp.dma_start(dst[:, HD * term:HD * (term + 1), c * CH:(c + 1) * CH],
                                         parts[n % 2][:, part, :]).then_inc(landed[n % 2], 16)

            def load_near(g, k):
                sp.dma_start(Qn[:, :, k * CH:(k + 1) * CH],
                             q_quad[bass.ds(g, 1), :, :, k * CH:(k + 1) * CH].rearrange("g p a t -> (g p) a t"))\
                  .then_inc(s_n[k], 16)
                load_keys(Kn, g, k, s_n[k])

            def load_keys(K, g, k, landed):
                for h in range(2):
                    p0 = ROWS * h
                    sp.dma_start(K[p0:p0 + ROWS, :, h, k * CH:(k + 1) * CH],
                                 k_quad[bass.ds(g, 1), p0:p0 + ROWS, :, k * CH:(k + 1) * CH]
                                 .rearrange("g p a t -> (g p) a t")).then_inc(landed, 16)

            def load_queries(g, k):
                sp.dma_start(Qr[:, :, (k - 2) * CH:(k - 1) * CH],
                             q_quad[bass.ds(g, 1), :, :, k * CH:(k + 1) * CH].rearrange("g p a t -> (g p) a t"))\
                  .then_inc(s_qr[k], 16)

            def place_max(L, g, c):
                G = QUADS * L + g
                sp.wait_ge(s_mrow, NC * G + c + 1)
                dst, at = q_src(c)
                for j in range(4):
                    p0 = ROWS * (j % 2) + MROW
                    sp.dma_start(dst[p0:p0 + 3, j // 2, at:at + CH], mrow[3 * j:3 * j + 3, c % 2, :])\
                      .then_inc(s_mq[c % 2], 16)

            def front(L, g):
                place_max(L, g, 2)
                place_max(L, g, 3)

            def back(L, g):
                at = NSTEP * (QUADS * L + g) + STEP0[3]
                sp.wait_ge(s_st, 4 * at)
                load_near(g + 1, 0)
                load_near(g + 1, 1)
                load_queries(g + 1, 2)
                sp.wait_ge(s_st, 4 * (at + 2))
                load_keys(Kr, g + 1, 0, s_kr[0])
                place_max(L, g + 1, 0)
                for k in (1, 2):
                    sp.wait_ge(s_st, 4 * (at + 2 * k + 2))
                    load_keys(Kr, g + 1, k, s_kr[k])
                place_max(L, g + 1, 1)
                sp.wait_ge(s_st, 4 * (at + STEPS[3]))
                load_keys(Kr, g + 1, 3, s_kr[3])
                load_queries(g + 1, 3)

            for L in range(2):
                store_parts(L)
                if L == 0:
                    sp.wait_ge(s_ones, 32)
                for landed in s_qst + s_kst:
                    sp.wait_ge(landed, 16 * 6 * 2 * (L + 1))
                load_near(0, 0)
                load_near(0, 1)
                load_queries(0, 2)
                for k in range(NC):
                    load_keys(Kr, 0, k, s_kr[k])
                load_queries(0, 3)
                place_max(L, 0, 0)
                place_max(L, 0, 1)
                front(L, 0)
                with sp.Fori(0, QUADS - 1) as g:
                    back(L, g)
                    front(L, g + 1)
            o_view = out[0].rearrange("(n p) d -> p n d", p=P)
            for c in range(NC):
                sp.wait_ge(s_ln, 3 * NC + c + 1)
                sp.dma_start(o_view[:, TPC * c:TPC * (c + 1), :], X[:, TPC * c:TPC * (c + 1), :]).then_inc(s_out, 16)
            sp.wait_ge(s_out, 16 * NC)

        @block.gpsimd
        def _(pool):
            pool.memset(fill[:, 0, :], 0.0).then_inc(s_cst, 1)
            pool.memset(fill[:, 1, :], 1.0).then_inc(s_cst, 1)
            pool.memset(mhalf[:, :], -0.5).then_inc(s_cst, 1)
            pool.memset(Vq[:, :, :, :], 0.0).then_inc(s_cst, 1)
            pool.wait_ge(s_cst, 4)
            pool.memset(Vq[:, :, :, HD:HD + 1], 1.0).then_inc(s_cst, 1)
            pool.dma_start(R[:, :, :].rearrange("p a b -> p (a b)"), rows.partition_broadcast(P)).then_inc(s_rows, 16)

            def add_bias(phase, name):
                for c in range(NC):
                    if phase:
                        pool.wait_ge(s_ln, NC * (phase - 1) + c + 1)
                    for i in range(TPC * c, TPC * (c + 1)):
                        ins = pool.tensor_tensor(XB[:, i, :], X[:, i, :], row(name), ALU.add)
                    ins.then_inc(s_xb, 1)

            def split_keys(L):
                for c in range(NC):
                    n = NC * L + c
                    pool.wait_ge(s_k1, n + 1)
                    pool.wait_ge(s_uk, n + 1)
                    pool.tensor_tensor(rk, uk, k_parts[n % 2][:, 0, :], ALU.subtract).then_inc(s_rk, 1)
                    pool.wait_ge(s_k2, n + 1)
                    pool.wait_ge(s_rk, n + 1)
                    pool.tensor_tensor(k_parts[n % 2][:, 2, :], rk, k_parts[n % 2][:, 1, :], ALU.subtract)\
                        .then_inc(s_k3, 1)

            def take_values(L, g, k):
                pool.tensor_copy(Vq[:, TPC * k:TPC * (k + 1), :, 0:HD],
                                 V[:, TPC * k:TPC * (k + 1), bass.ds(4 * g, 4), :]).then_inc(s_vq, 1)

            def attention(L):
                for k in range(NC):
                    pool.wait_ge(s_took, NC * L + k + 1)
                    take_values(L, 0, k)
                with pool.Fori(0, QUADS - 1) as g:
                    for k in range(NC):
                        pool.wait_ge(s_pv, NSTEP * (QUADS * L + g) + STEP0[3] + 2 * k + 2)
                        take_values(L, g + 1, k)

            def powers(phase):
                for c in range(NC):
                    n = NC * phase + c
                    pool.wait_ge(s_mv, n + 1)
                    pool.tensor_scalar(veps[:, n % 2, :], mean_var[:, n % 2, :, 1], EPS, None, ALU.add).then_inc(s_ve, 1)
                    pool.wait_ge(s_ve, n + 1)
                    pool.tensor_tensor(rstd[:, n % 2, :], veps[:, n % 2, :], mhalf[:, :], ALU.pow).then_inc(s_rs, 1)

            split_keys(0)
            pool.wait_ge(s_x, 16)
            pool.wait_ge(s_rows, 16)
            add_bias(0, "bo")
            attention(0)
            powers(0)
            add_bias(1, "b2")
            powers(1)
            add_bias(2, "bo1")
            split_keys(1)
            attention(1)
            powers(2)
            powers(3)

        @block.tensor
        def _(pe):
            def project(L):
                for c in range(NC):
                    n = NC * L + c
                    xt = XT[:, c * CH:(c + 1) * CH]
                    if L == 0:
                        if c == 0:
                            pe.wait_ge(s_w1, 32)
                    else:
                        pe.wait_ge(s_xt, NC + c + 1)
                    if c == 0 and L:
                        pe.wait_ge(s_hr, KH * NC)
                    if n:
                        pe.wait_ge(s_uq, n)
                    if L:
                        pe.matmul(half[0], w("Wq1"), xt, start=True, stop=True).then_inc(s_proj, 1)
                    else:
                        pe.matmul(half[0], w("Wq"), xt, start=True, stop=True)
                        pe.matmul(half[1], w("Wqs"), xt, start=True, stop=True).then_inc(s_proj, 1)
                    if n:
                        pe.wait_ge(s_uk, n)
                    if L:
                        pe.matmul(half[2], w("Wk1"), xt, start=True, stop=True).then_inc(s_proj, 1)
                    else:
                        pe.matmul(half[2], w("Wk"), xt, start=True, stop=True)
                        pe.matmul(half[3], w("Wks"), xt, start=True, stop=True).then_inc(s_proj, 1)
                    if n:
                        pe.wait_ge(s_took, n)
                    if L and c == 0:
                        pe.wait_ge(s_yr, 2 * NC)
                    for i in range(TPC):
                        mm = pe.matmul(MX[:, 0, i * P:(i + 1) * P], XT[:, c * CH + i * P:c * CH + (i + 1) * P],
                                       w("Wv1" if L else "Wv"), start=True, stop=True)
                    mm.then_inc(s_proj, 1)

            def max_block(L, g, c, b):
                n = NMAX * (QUADS * L + g) + MAX0[c] + b
                j, i, k = b % 4, (b // 4) % TPC, b // (4 * TPC)
                Q, at = q_src(c)
                K = Kr if c >= 2 else Kn
                if b == 0 and c >= 2:
                    pe.wait_ge(s_qr[c], 16 * (QUADS * L + g + 1))
                if b == 0 and c == 1:
                    pe.wait_ge(s_n[c], 48 * (QUADS * L + g + 1))
                if b % (4 * TPC) == 0 and (c, k) != (1, 1):
                    pe.wait_ge(s_kr[k] if c >= 2 else s_n[k], (32 if c >= 2 else 48) * (QUADS * L + g + 1))
                if not (c == 0 and b < 2 and L == 0 and isinstance(g, int) and g == 0):
                    pe.wait_ge(s_red, n - 1)
                diag = k == c
                width = (i + 1) * P if diag else CH
                mm = pe.matmul(MX[:, b % 2, 0:width], Q[:, j // 2, at + i * P:at + (i + 1) * P],
                               K[:, j // 2, j % 2, k * CH:k * CH + width], start=True, stop=not diag)
                if diag:
                    mm = pe.matmul(MX[:, b % 2, i * P:(i + 1) * P], ident16[:, :], mask_ts[:, :], start=False,
                                   stop=True)
                mm.then_inc(s_max, 1)

            def max_rows(L, g, c):
                n = NC * (QUADS * L + g) + c
                pe.wait_ge(s_nmax, n + 1)
                pe.wait_ge(s_mrow, n)
                for i in range(TPC):
                    mm = pe.matmul(MT[0:12, i * P:(i + 1) * P],
                                   nmax[:, c % 2, 4 * i:4 * i + 4, :].rearrange("p j k -> p (j k)"), ident16[:, :],
                                   start=True, stop=True)
                mm.then_inc(s_mtp, 1)

            def scores(L, g, c, s, j, pace):
                u = STEP0[c] + s
                idx = 4 * (NSTEP * (QUADS * L + g) + u) + j
                Q, at = q_src(c)
                K = Kr if c >= 2 else Kn
                if s == 0 and j == 0:
                    pe.wait_ge(s_mq[c % 2], 64 * (2 * (QUADS * L + g) + c // 2 + 1))
                if c == 0 and L == 0 and s == 0 and isinstance(g, int) and j < 2:
                    pass
                else:
                    pe.wait_ge(s_exp, idx - 1)
                for tile, t0, col in GROUPS[c][s]:
                    diag = tile >= TPC * c
                    dst = ST[:, j % 2, col:col + CH - t0]
                    mm = pe.matmul(dst, K[:, j // 2, j % 2, tile * P:(tile + 1) * P],
                                   Q[:, j // 2, at + t0:at + CH], start=True, stop=not diag)
                    if diag:
                        mm = pe.matmul(ST[:, j % 2, col:col + P], ident16[:, :], mask_st[:, :], start=False, stop=True)
                    if tile == GROUPS[c][s][-1][0]:
                        mm.then_inc(s_st, 1)
                    pace(CH - t0)

            def sums(L, g, c, s, pace):
                G = QUADS * L + g
                u = STEP0[c] + s
                if s == 0:
                    if c or not isinstance(g, int) or G:
                        pe.wait_ge(s_oe, NC * G + c)
                    pe.wait_ge(s_vq, NC * G + c + 1)
                pe.wait_ge(s_exp, 4 * (NSTEP * G + u + 1))
                for tile, t0, col in GROUPS[c][s]:
                    for j in range(4):
                        mm = pe.matmul(OT[32 * j:32 * j + 32, t0:CH], Vq[:, tile, j, :],
                                       probs[:, 4 * (u % 2) + j, col:col + CH - t0], start=(tile == 0),
                                       stop=(s == STEPS[c] - 1 and tile == GROUPS[c][s][-1][0]), skip_group_check=True)
                    if tile == GROUPS[c][s][-1][0]:
                        mm.then_inc(s_pv, 1)
                    pace(4 * (CH - t0))

            def step(L, g, u, before, more):
                c = max(c for c in range(NC) if STEP0[c] <= u)
                s = u - STEP0[c]
                lo = max(k for k in BLOCKS_BY if k <= u)
                hi = min(k for k in BLOCKS_BY if k > u)
                widths = [step_width(GROUPS[cc][ss]) for cc in range(NC) for ss in range(STEPS[cc])]
                span = sum(widths[lo:hi])
                first = BLOCKS_BY[lo] + (BLOCKS_BY[hi] - BLOCKS_BY[lo]) * sum(widths[lo:u]) // span
                last = BLOCKS_BY[lo] + (BLOCKS_BY[hi] - BLOCKS_BY[lo]) * sum(widths[lo:u + 1]) // span
                total = 4 * widths[u] + (4 * step_width(GROUPS[before[1]][before[2]]) if before else 0)
                spent = [0, first]

                def pace(columns):
                    spent[0] += columns
                    upto = first + (last - first) * spent[0] // total
                    for b in range(spent[1], upto):
                        ahead, cc, block = STREAM[b]
                        if more or not ahead:
                            max_block(L, g + ahead, cc, block)
                    spent[1] = upto

                scores(L, g, c, s, 0, pace)
                scores(L, g, c, s, 1, pace)
                if u in ROWS_AT and (more or not ROWS_AT[u][0]):
                    max_rows(L, g + ROWS_AT[u][0], ROWS_AT[u][1])
                if before:
                    sums(L, *before, pace)
                scores(L, g, c, s, 2, pace)
                scores(L, g, c, s, 3, pace)
                return g, c, s

            def front(L, g, before):
                for u in range(STEP0[3]):
                    before = step(L, g, u, before, True)
                return before

            def back(L, g, before, more):
                for u in range(STEP0[3], NSTEP):
                    before = step(L, g, u, before, more)
                return before

            def attention(L):
                for c in (0, 1):
                    for b in range(MAXB[c]):
                        max_block(L, 0, c, b)
                    max_rows(L, 0, c)
                front(L, 0, None)
                with pe.Fori(0, QUADS - 1) as g:
                    before = back(L, g, (g, 2, STEPS[2] - 1), True)
                    front(L, g + 1, before)
                before = back(L, QUADS - 1, (QUADS - 1, 2, STEPS[2] - 1), False)
                sums(L, *before, lambda columns: None)

            def turned_sums(L):
                pe.wait_ge(s_oe, NC * QUADS * (L + 1))
                pe.wait_ge(s_exp, 4 * NSTEP * QUADS * (L + 1))
                pe.wait_ge(s_red, NMAX * QUADS * (L + 1))
                for step in range(NT + 2):
                    if step < NT:
                        n = NT * L + step
                        if n >= 2:
                            pe.wait_ge(s_attn, n - 1)
                        for g in range(QUADS):
                            mm = pe.transpose(half[n % 2][:, g * P:(g + 1) * P], O[:, g, step * P:(step + 1) * P],
                                              w("ident"))
                        mm.then_inc(s_turn, 1)
                    if 1 <= step <= NT:
                        n = NT * L + step - 1
                        pe.wait_ge(s_attn, n + 1)
                        if n >= 2:
                            pe.wait_ge(s_ate, n - 1)
                        pe.transpose(half[2 + n % 2][:, 0:P], attn[:, n % 2, :], w("ident")).then_inc(s_atp, 1)
                    if step >= 2:
                        tile = step - 2
                        n = NT * L + tile
                        c, i = divmod(tile, TPC)
                        ln = 2 * NC * L + c
                        pe.wait_ge(s_ate, n + 1)
                        if i == 0 and ln >= 2:
                            pe.wait_ge(s_yr, ln - 1)
                        pe.matmul(MX[:, c % 2, i * P:(i + 1) * P], attnT[:, n % 2, :], w("Wo1" if L else "Wo"),
                                  start=True, stop=True).then_inc(s_wo, 1)
                    if step >= 9 and (step - 9) % TPC == 0:
                        channels(2 * NC * L + (step - 9) // TPC)
                channels(2 * NC * L + NC - 1)

            def channels(ln):
                pe.wait_ge(s_ln, ln + 1)
                pe.wait_ge(s_xt, ln)
                if ln % NC == 0:
                    pe.wait_ge(s_mrow, NC * QUADS * (ln // (2 * NC) + 1))
                c = ln % NC
                for i in range(TPC):
                    mm = pe.transpose(MT[:, i * P:(i + 1) * P], X[:, TPC * c + i, :], w("ident"))
                mm.then_inc(s_xtp, 1)

            def out_product(ln, slot, weight):
                c = ln % NC
                pe.wait_ge(s_yr, ln - 1)
                for i in range(TPC):
                    for k in range(KH):
                        mm = pe.matmul(MX[:, c % 2, i * P:(i + 1) * P], hid[:, slot, k, i * P:(i + 1) * P],
                                       w(weight, k, D), start=(k == 0), stop=(k == KH - 1))
                mm.then_inc(s_y, 1)

            def mlp0():
                pe.wait_ge(s_ate, NT)
                for step in range(NC + 2):
                    if step < NC:
                        pe.wait_ge(s_xt, step + 1)
                        for m in range(KH):
                            n = KH * step + m
                            if n >= 2:
                                pe.wait_ge(s_hr, n - 1)
                            pe.matmul(half[n % 2], w("W1", m, P), XT[:, step * CH:(step + 1) * CH],
                                      start=True, stop=True).then_inc(s_ha, 1)
                    if 1 <= step <= NC:
                        pe.wait_ge(s_hr, KH * step)
                        out_product(NC + step - 1, step - 1, "W2")
                    if step >= 2:
                        channels(NC + step - 2)

            def mlp1():
                pe.wait_ge(s_ate, 2 * NT)
                for kind, c in MLP1:
                    if kind == "out":
                        pe.wait_ge(s_hr, mlp1_index("h2", c) + KH)
                        out_product(3 * NC + c, c % 2, "W3")
                        continue
                    at = mlp1_index(kind, c)
                    if kind == "gate":
                        pe.wait_ge(s_xt, 2 * NC + c + 1)
                    elif kind == "h1":
                        pe.wait_ge(s_hm, KH * (c + 1))
                    else:
                        pe.wait_ge(s_hr, mlp1_index("h1", c) + KH)
                    for m in range(KH):
                        n = at + m
                        pe.wait_ge(s_hr, n - 1)
                        if kind == "gate":
                            pe.matmul(half[n % 2], w("A", m, P), XT[:, c * CH:(c + 1) * CH], start=True, stop=True)\
                              .then_inc(s_ha, 1)
                            b = KH * c + m
                            if b >= 2:
                                pe.wait_ge(s_hm, b - 1)
                            pe.matmul(half[2 + b % 2], w("B", m, P), XT[:, c * CH:(c + 1) * CH], start=True, stop=True)\
                              .then_inc(s_hb, 1)
                        else:
                            slot = c % 2 if kind == "h1" else 2 + c % 2
                            weight = "H1" if kind == "h1" else "H2"
                            for k in range(KH):
                                mm = pe.matmul(half[n % 2], w(weight, k, HID)[:, m * P:(m + 1) * P], hid[:, slot, k, :],
                                               start=(k == 0), stop=(k == KH - 1))
                            mm.then_inc(s_ha, 1)

            for L in range(2):
                project(L)
                if L == 0:
                    pe.wait_ge(s_rest, 16)
                    pe.wait_ge(s_c16, 7)
                    pe.wait_ge(s_cst, 5)
                pe.wait_ge(s_uk, NC * (L + 1))
                pe.wait_ge(s_took, NC * (L + 1))
                attention(L)
                turned_sums(L)
                (mlp1 if L else mlp0)()

        @block.scalar
        def _(act):
            def split(L):
                for c in range(NC):
                    n = NC * L + c
                    for u, r, parts, ready, rest, one, two, landed, scale in (
                            (uq, rq, q_parts, s_uq, s_rq, s_q1, s_q2, s_qst, SCALE),
                            (uk, rk, k_parts, s_uk, s_rk, s_k1, s_k2, s_kst, 1.0)):
                        act.wait_ge(ready, n + 1)
                        if n >= 2:
                            act.wait_ge(landed[n % 2], 96 * (n // 2))
                        act.activation(parts[n % 2][:, 0, :], u, ACT.Copy, scale=scale).then_inc(one, 1)
                        act.wait_ge(rest, n + 1)
                        act.activation(parts[n % 2][:, 1, :], r, ACT.Copy).then_inc(two, 1)
                    if L == 0 and c + 2 < NC:
                        load_angles(c + 2)

            def keep_rows(L, g, c):
                n = NC * (QUADS * L + g) + c
                act.wait_ge(s_mtp, n + 1)
                act.activation(mrow[:, c % 2, :], MT[0:12, :], ACT.Copy).then_inc(s_mrow, 1)

            def keep_sums(L, g, c):
                act.wait_ge(s_pv, NSTEP * (QUADS * L + g) + STEP0[c] + STEPS[c])
                act.activation(O[:, bass.ds(g, 1), c * CH:(c + 1) * CH].rearrange("p g t -> p (g t)"), OT[:, :],
                               ACT.Copy).then_inc(s_oe, 1)

            def chunk(L, g, c, first=False, more=True):
                G = QUADS * L + g
                for s in range(STEPS[c]):
                    u = STEP0[c] + s
                    width = step_width(GROUPS[c][s])
                    for j in range(4):
                        if j == 2 and s == 0 and not first:
                            keep_sums(L, *((g, c - 1) if c else (g - 1, NC - 1)))
                        if j == 2 and u in ROWS_AT and (more or not ROWS_AT[u][0]):
                            keep_rows(L, g + ROWS_AT[u][0], ROWS_AT[u][1])
                        act.wait_ge(s_st, 4 * (NSTEP * G + u) + j + 1)
                        if not (first and s < 2):
                            act.wait_ge(s_pv, NSTEP * G + u - 1)
                        act.activation(probs[:, 4 * (u % 2) + j, 0:width], ST[:, j % 2, 0:width], ACT.Exp)\
                           .then_inc(s_exp, 1)

            def front(L, g, first):
                chunk(L, g, 0, first)
                chunk(L, g, 1)
                chunk(L, g, 2)

            def keep_channels(ln):
                act.wait_ge(s_xtp, ln + 1)
                c = ln % NC
                act.activation(XT[:, c * CH:(c + 1) * CH], MT[:, :], ACT.Copy).then_inc(s_xt, 1)

            def keep_attention(L):
                for tile in range(NT):
                    n = NT * L + tile
                    act.wait_ge(s_atp, n + 1)
                    if n >= 2:
                        act.wait_ge(s_wo, n - 1)
                    act.activation(attnT[:, n % 2, :], half[2 + n % 2][:, 0:P], ACT.Copy).then_inc(s_ate, 1)
                    if tile >= 8 and (tile - 8) % TPC == 0:
                        keep_channels(2 * NC * L + (tile - 8) // TPC)
                for c in (2, 3):
                    keep_channels(2 * NC * L + c)

            def mlp0():
                for step in range(NC + 2):
                    if step < NC:
                        for m in range(KH):
                            n = KH * step + m
                            act.wait_ge(s_ha, n + 1)
                            act.activation(hid[:, step, m, :], half[n % 2], ACT.Gelu,
                                           bias=w("b1", m, 1)).then_inc(s_hr, 1)
                    if step >= 2:
                        keep_channels(NC + step - 2)

            def mlp1():
                for kind, c in MLP1:
                    if kind == "out":
                        continue
                    at = mlp1_index(kind, c)
                    if kind == "gate" and c >= 2:
                        act.wait_ge(s_y, NC + c - 1)
                    for m in range(KH):
                        n = at + m
                        act.wait_ge(s_ha, n + 1)
                        if kind == "gate":
                            act.activation(hid[:, c % 2, m, :], half[n % 2], ACT.Silu,
                                           scale=w("sa", m, 1)).then_inc(s_hr, 1)
                        elif kind == "h1":
                            act.activation(hid[:, 2 + c % 2, m, :], half[n % 2], ACT.Gelu,
                                           scale=w("s1", m, 1)).then_inc(s_hr, 1)
                        else:
                            act.activation(hid[:, c % 2, m, :], half[n % 2], ACT.Gelu,
                                           scale=w("s2", m, 1)).then_inc(s_hr, 1)

            def load_angles(c):
                if c >= 2:
                    act.wait_ge(s_rot, 2 * (c - 2) + 2)
                for f, table in enumerate((cos, sin)):
                    act.dma_start(angles[:, c % 2, f, :], table[:, c * CH:(c + 1) * CH]).then_inc(s_ang[c % 2], 16)

            load_angles(0)
            load_angles(1)
            for L in range(2):
                split(L)
                keep_rows(L, 0, 0)
                keep_rows(L, 0, 1)
                front(L, 0, True)
                with act.Fori(0, QUADS - 1) as g:
                    chunk(L, g, 3)
                    front(L, g + 1, False)
                chunk(L, QUADS - 1, 3, more=False)
                keep_sums(L, QUADS - 1, NC - 1)
                keep_attention(L)
                (mlp1 if L else mlp0)()

        @block.vector
        def _(dve):
            def project(L):
                for c in range(NC):
                    n = NC * L + c
                    if L == 0:
                        dve.wait_ge(s_ang[c % 2], 32 * (c // 2 + 1))
                    for qk, (u, t, r, ready, b) in enumerate(((uq, tq, rq, s_uq, "bq"), (uk, tk, rk, s_uk, "bk"))):
                        dve.wait_ge(s_proj, 3 * n + qk + 1)
                        if n:
                            dve.wait_ge(s_k3 if qk else s_q3, n)
                        if L == 0:
                            dve.scalar_tensor_tensor(u, half[2 * qk], w(b), angles[:, c % 2, 0, :], ALU.add, ALU.mult)
                            dve.scalar_tensor_tensor(t, half[2 * qk + 1], w(b + "s"), angles[:, c % 2, 1, :], ALU.add,
                                                     ALU.mult).then_inc(s_rot, 1)
                            dve.wait_ge(s_rot, 2 * n + qk + 1)
                            dve.tensor_tensor(u, u, t, ALU.add).then_inc(ready, 1)
                        else:
                            dve.tensor_copy(u, half[2 * qk]).then_inc(ready, 1)
                    dve.wait_ge(s_proj, 3 * n + 3)
                    dst = V[:, TPC * c:TPC * (c + 1), :, :].rearrange("p n h d -> p n (h d)")
                    src = MX[:, 0, :].rearrange("p (n e) -> p n e", n=TPC)
                    if L == 0:
                        dve.tensor_tensor(dst, src, row("bv").unsqueeze(1).to_broadcast([P, TPC, D]), ALU.add)\
                           .then_inc(s_took, 1)
                    else:
                        dve.tensor_copy(dst, src).then_inc(s_took, 1)
                    dve.wait_ge(s_q1, n + 1)
                    dve.wait_ge(s_uq, n + 1)
                    dve.scalar_tensor_tensor(rq, uq, SCALE, q_parts[n % 2][:, 0, :], ALU.mult, ALU.subtract)\
                       .then_inc(s_rq, 1)
                    dve.wait_ge(s_q2, n + 1)
                    dve.wait_ge(s_rq, n + 1)
                    dve.tensor_tensor(q_parts[n % 2][:, 2, :], rq, q_parts[n % 2][:, 1, :], ALU.subtract)\
                       .then_inc(s_q3, 1)

            def max_chunk(L, g, c):
                G = QUADS * L + g
                for b in range(MAXB[c]):
                    n = NMAX * G + MAX0[c] + b
                    j, i, k = b % 4, (b // 4) % TPC, b // (4 * TPC)
                    width = (i + 1) * P if k == c else CH
                    dve.wait_ge(s_max, n + 1)
                    dve.reduce_max(maxp[:, c % 2, 4 * i + j, k:k + 1], MX[:, b % 2, 0:width], AX_X).then_inc(s_red, 1)
                n = NC * G + c
                dve.wait_ge(s_red, NMAX * G + MAX0[c] + MAXB[c])
                dve.reduce_max(mx[:, c % 2, :], maxp[:, c % 2, :, 0:c + 1], AX_X).then_inc(s_comb, 1)
                dve.wait_ge(s_comb, 4 * n + 1)
                nm = nmax[:, c % 2, :, :]
                dve.tensor_scalar(nm[:, :, 0], mx[:, c % 2, :], -1.0, None, ALU.mult).then_inc(s_comb, 1)
                dve.wait_ge(s_comb, 4 * n + 2)
                dve.scalar_tensor_tensor(mres[:, c % 2, :], mx[:, c % 2, :], -1.0, nm[:, :, 0], ALU.mult, ALU.subtract)\
                   .then_inc(s_comb, 1)
                dve.wait_ge(s_comb, 4 * n + 3)
                dve.tensor_copy(nm[:, :, 1], mres[:, c % 2, :]).then_inc(s_comb, 1)
                dve.wait_ge(s_comb, 4 * n + 4)
                dve.tensor_tensor(nm[:, :, 2], mres[:, c % 2, :], nm[:, :, 1], ALU.subtract).then_inc(s_nmax, 1)

            def branch(ln, product_done, count):
                c = ln % NC
                y = Y[:, ln % 2, :, :]
                bank = MX[:, c % 2, :].rearrange("p (n e) -> p n e", n=TPC)
                dve.wait_ge(product_done, count)
                if ln < 3 * NC:
                    dve.wait_ge(s_xb, ln + 1)
                    dve.tensor_tensor(y, bank, XB[:, TPC * c:TPC * (c + 1), :], ALU.add).then_inc(s_yr, 1)
                else:
                    dve.tensor_tensor(y, bank, row("s3").unsqueeze(1).to_broadcast([P, TPC, D]), ALU.mult)\
                       .then_inc(s_t3, 1)
                    dve.wait_ge(s_t3, c + 1)
                    dve.tensor_tensor(y, y, X[:, TPC * c:TPC * (c + 1), :], ALU.add).then_inc(s_yr, 1)
                dve.wait_ge(s_yr, ln + 1)
                for i in range(TPC):
                    ins = dve.bn_stats(stats[:, ln % 2, i, :], Y[:, ln % 2, i, :])
                ins.then_inc(s_bn, 1)
                dve.wait_ge(s_bn, ln + 1)
                for i in range(TPC):
                    ins = dve.bn_aggr(mean_var[:, ln % 2, i, :], stats[:, ln % 2, i, :])
                ins.then_inc(s_mv, 1)

            def normalise(ln):
                c = ln % NC
                dve.wait_ge(s_rs, ln + 1)
                for i in range(TPC):
                    ins = dve.tensor_scalar(X[:, TPC * c + i, :], Y[:, ln % 2, i, :], mean_var[:, ln % 2, i, 0:1],
                                            rstd[:, ln % 2, i:i + 1], ALU.subtract, ALU.mult)
                ins.then_inc(s_ln, 1)

            def attention_out(L):
                for tile in range(NT):
                    n = NT * L + tile
                    dve.wait_ge(s_turn, n + 1)
                    bank = half[n % 2].rearrange("p (h e) -> p h e", h=H)
                    dve.reciprocal(rden[:, n % 2, :], bank[:, :, HD]).then_inc(s_rden, 1)
                    dve.wait_ge(s_rden, n + 1)
                    if n >= 2:
                        dve.wait_ge(s_atp, n - 1)
                    dve.tensor_tensor(attn[:, n % 2, :].rearrange("p (h e) -> p h e", h=H), bank[:, :, 0:HD],
                                      rden[:, n % 2, :].unsqueeze(2).to_broadcast([P, H, HD]), ALU.mult)\
                       .then_inc(s_attn, 1)
                    if tile >= 5 and (tile - 5) % TPC == 0:
                        c = (tile - 5) // TPC
                        branch(2 * NC * L + c, s_wo, NT * L + TPC * (c + 1))
                    if tile >= 7 and (tile - 7) % TPC == 0:
                        normalise(2 * NC * L + (tile - 7) // TPC)
                branch(2 * NC * L + 3, s_wo, NT * (L + 1))
                normalise(2 * NC * L + 3)

            def mlp0():
                for c in range(NC + 1):
                    if c < NC:
                        branch(NC + c, s_y, c + 1)
                    if c:
                        normalise(NC + c - 1)

            def mlp1():
                for kind, c in MLP1:
                    if kind == "gate":
                        for m in range(KH):
                            b = KH * c + m
                            dve.wait_ge(s_hb, b + 1)
                            dve.wait_ge(s_hr, mlp1_index("gate", c) + m + 1)
                            h = hid[:, c % 2, m, :]
                            dve.scalar_tensor_tensor(h, half[2 + b % 2], w("sb", m, 1), h, ALU.mult, ALU.mult)\
                               .then_inc(s_hm, 1)
                    if kind == "out":
                        branch(3 * NC + c, s_y, NC + c + 1)
                        normalise(3 * NC + c)

            for K in (Kn, Kr):
                for h in range(2):
                    dve.memset(K[ROWS * (1 - h):ROWS * (2 - h), :, h, :], 0.0).then_inc(s_c16, 1)
            dve.wait_ge(s_w1, 32)
            dve.tensor_copy(ident16[:, :], w("ident")).then_inc(s_c16, 1)
            dve.wait_ge(s_rows, 16)
            for L in range(2):
                project(L)
                if L == 0:
                    dve.wait_ge(s_rest, 16)
                    dve.tensor_copy(mask_ts[:, :], w("mask_ts")).then_inc(s_c16, 1)
                    dve.tensor_copy(mask_st[:, :], w("mask_st")).then_inc(s_c16, 1)
                max_chunk(L, 0, 0)
                for c in range(1, NC):
                    max_chunk(L, 0, c)
                with dve.Fori(0, QUADS - 1) as g:
                    for c in range(NC):
                        max_chunk(L, g + 1, c)
                attention_out(L)
                (mlp1 if L else mlp0)()


def kernel(**inputs):
    import numpy as np
    import concourse.bacc as bacc
    from concourse import mybir as mb
    from concourse.bass_utils import run_bass_kernel_spmd

    a = {k: np.ascontiguousarray(v) for k, v in inputs.items()}
    pair = np.arange(D) ^ 1
    spread = (np.arange(H) // 4)[:, None] * HD + np.arange(HD)[None]
    spread = spread.reshape(-1)

    def tiles(m):
        return m.reshape(-1, P, m.shape[1]).transpose(1, 0, 2).reshape(P, -1)

    def cols(v):
        return v.reshape(-1, P).T

    low = np.float32(-1e30)
    later = np.arange(P)[None, :] > np.arange(P)[:, None]
    freq = np.exp(-(np.arange(0, HD, 2, dtype=np.float32) / np.float32(HD)) * np.log(np.float32(10000.0)))
    angle = np.arange(T, dtype=np.float32)[None, :] * freq.astype(np.float32)[(np.arange(D) % HD) // 2][:, None]
    sign = np.where(np.arange(D) % 2 == 0, -1.0, 1.0)[:, None]
    cos = np.cos(angle.astype(np.float64)).astype(np.float32)
    sin = (np.sin(angle.astype(np.float64)) * sign).astype(np.float32)

    Wk, Wv = a["L0_attn_Wk"][:, spread], a["L0_attn_Wv"][:, spread]
    bk, bv = a["L0_attn_bk"][spread], a["L0_attn_bv"][spread]
    m = {
        "Wq": a["L0_attn_Wq"], "Wqs": a["L0_attn_Wq"][:, pair], "Wk": Wk, "Wks": Wk[:, pair], "Wv": Wv,
        "ident": np.eye(P, dtype=np.float32),
        "bq": cols(a["L0_attn_bq"]), "bqs": cols(a["L0_attn_bq"][pair]), "bk": cols(bk), "bks": cols(bk[pair]),
        "mask_ts": np.where(later, low, np.float32(0)), "mask_st": np.where(later.T, low, np.float32(0)),
        "Wo": a["L0_attn_Wo"], "W1": a["L0_ffn_w1"], "W2": tiles(a["L0_ffn_w2"]),
        "Wq1": a["L1_attn_Wq"], "Wk1": a["L1_attn_Wk"], "Wv1": a["L1_attn_Wv"], "Wo1": a["L1_attn_Wo"],
        "A": a["L1_ffn_w1_w"].T, "B": a["L1_ffn_w2_w"].T, "H1": tiles(a["L1_ffn_h1_w"].T),
        "H2": tiles(a["L1_ffn_h2_w"].T), "W3": tiles(a["L1_ffn_w3_w"].T),
        "b1": cols(a["L0_ffn_b1"]), "sa": cols(a["L1_ffn_w1_s"]), "sb": cols(a["L1_ffn_w2_s"]),
        "s1": cols(a["L1_ffn_h1_s"]), "s2": cols(a["L1_ffn_h2_s"]),
    }
    pack = np.zeros((P, PACK_W), np.float32)
    for name, (at, width) in OFF.items():
        pack[:, at:at + width] = m[name]
    rows = np.concatenate([bv, a["L0_attn_bo"], a["L0_ffn_b2"], a["L1_attn_bo"], a["L1_ffn_w3_s"]])[None, :]
    arrays = {"x_in": a["L0_attn_x"], "xT_in": np.ascontiguousarray(a["L0_attn_x"][0].T), "pack": pack, "rows": rows,
              "cos": cos, "sin": sin}
    nc = bacc.Bacc("TRN2", target_bir_lowering=False, num_devices=1)
    args = [nc.dram_tensor(k, v.shape, mb.dt.from_np(v.dtype), kind="ExternalInput").ap() for k, v in arrays.items()]
    args.append(nc.dram_tensor("y_out", (1, T, D), mb.dt.float32, kind="ExternalOutput").ap())
    program(nc, *args)
    r = run_bass_kernel_spmd(nc, [arrays], core_ids=[0])
    return r.results[0]["y_out"]
```

```python
from contextlib import ExitStack

import concourse.bass as bass
from concourse import mybir

F32 = mybir.dt.float32
BF16 = mybir.dt.bfloat16
ALU = mybir.AluOpType
ACT = mybir.ActivationFunctionType
AX_X = mybir.AxisListType.X

T = 2048
D = 128
H = 16
HD = D // H
P = 128
CH = 512
NC = T // CH
TPC = CH // P
NT = T // P
QUADS = H // 4
HID = 512
KH = HID // P
ROWS = 64
TERMS = 6
MROW = TERMS * HD
RUNS = ((0, 3, 0, 0), (3, 2, 1, 0), (5, 1, 2, 0))
SCALE = float(HD) ** -0.5
EPS = 1e-5

FIRST = ["Wq", "Wqs", "Wk", "Wks", "Wv", "ident"]
FIRST_W = [D, D, D, D, D, P]
VEC = ["bq", "bqs", "bk", "bks"]
MASKS = ["mask_ts"]
REST = ["Wo", "W1", "W2", "Wq1", "Wk1", "Wv1", "Wo1", "A", "B", "H1", "H2", "W3"]
REST_W = [D, HID, KH * D, D, D, D, D, HID, HID, KH * HID, KH * HID, KH * D]
COLS = ["b1", "sa", "sb", "s1", "s2"]


def offsets():
    at, off = 0, {}
    for n, w in list(zip(FIRST, FIRST_W)) + [(n, 1) for n in VEC]:
        off[n] = (at, w)
        at += w
    first = at
    for n in MASKS:
        off[n] = (at, P)
        at += P
    for n, w in list(zip(REST, REST_W)) + [(n, KH) for n in COLS]:
        off[n] = (at, w)
        at += w
    return off, first, first + P * len(MASKS), at


OFF, FIRST_END, MASKS_END, PACK_W = offsets()
ROWV = ["bv", "bo", "b2", "bo1", "s3"]

def steps_of(c):
    full = [[(tile, 0, 0)] for tile in range(TPC * c)]
    diag = [[(TPC * c, 0, 0)], [(TPC * c + 1, P, 0), (TPC * c + 3, 3 * P, 3 * P)], [(TPC * c + 2, 2 * P, 0)]]
    return full + (diag[::-1] if c else diag)


STEPS = [(c, tiles) for c in range(NC) for tiles in steps_of(c)]
NSTEP = len(STEPS)
STEP0 = [min(u for u in range(NSTEP) if STEPS[u][0] == c) for c in range(NC)]
LAST = [u for u in range(NSTEP) if u + 1 == NSTEP or STEPS[u + 1][0] != STEPS[u][0]]
WIDTH = [sum(CH - t0 for _, t0, _ in tiles) for _, tiles in STEPS]
DIAG = [u for u in range(NSTEP) if STEPS[u][1][0][0] >= TPC * STEPS[u][0]]
LAG = 2
SLOTS = 4
RING = 3


def blocks_of(c):
    full = [(i, j, 1, k, CH) for k in range(c) for i in range(TPC) for j in range(4)]
    return full + [(i, j, n, c, (i + 1) * P) for i, n in ((0, 4), (1, 2), (2, 1), (3, 1)) for j in range(0, 4, n)]


BLOCKS = [(c, *block) for c in range(NC) for block in blocks_of(c)]
NMAX = len(BLOCKS)
MAX_END = [max(b for b in range(NMAX) if BLOCKS[b][0] == c) + 1 for c in range(NC)]

TURN = STEP0[3] - 3


def blocks_done():
    cost = [n * width + P // 2 for _, _, _, n, _, width in BLOCKS]
    share = [sum(cost[:n]) / sum(cost) for n in range(NMAX + 1)]
    done = []
    for u in range(NSTEP + 1):
        passed = WIDTH[TURN:u] if u > TURN else WIDTH[TURN:] + WIDTH[:u]
        part = sum(passed) / sum(WIDTH)
        done.append(max(n for n in range(NMAX + 1) if share[n] <= part + 1e-9))
    return done


DONE = blocks_done()
ROWS_AT = {min(u for u in range(TURN + 1, NSTEP) if DONE[u] >= MAX_END[0]) + 1: (1, 0),
           max(STEP0[3] + 1, min(u for u in range(TURN + 1, NSTEP) if DONE[u] >= MAX_END[1]) + 1): (1, 1),
           min(u for u in range(NSTEP) if DONE[u] >= MAX_END[2]) + 2: (0, 2), TURN: (0, 3)}
CUT = STEP0[2] + TPC


def start_done():
    ends = [(0, MAX_END[1] - 6), (1, MAX_END[1]), (STEP0[2] - 3, MAX_END[2]), (CUT, DONE[CUT])]
    return [a + (b - a) * (u - u0) // (u1 - u0) for (u0, a), (u1, b) in zip(ends, ends[1:]) for u in range(u0, u1)] + \
        [DONE[CUT]]


START_DONE = start_done()
START_ROWS_AT = {1: (0, 1), STEP0[2] - 3: (0, 2)}
OUT_STEP = TURN + 1
EARLY = TPC * (NC - 1)

MLP1 = [("gate", 0), ("gate", 1), ("turn", 3), ("h1", 0), ("h1", 1), ("h2", 0), ("h2", 1), ("out", 0), ("gate", 2),
        ("out", 1), ("gate", 3), ("h1", 2), ("h1", 3), ("h2", 2), ("h2", 3), ("out", 2), ("out", 3)]


def mlp1_index(kind, c):
    before = MLP1[:MLP1.index((kind, c))]
    return KH * NC + KH * len([k for k, _ in before if k not in ("out", "turn")])


def program(nc, x_in, xT_in, pack, rows, cos, sin, out):
    with ExitStack() as ctx:
        def sb(name, shape, dt=F32):
            return ctx.enter_context(nc.sbuf_tensor(name, shape, dt))

        def psum(name, shape):
            return ctx.enter_context(nc.psum_tensor(name, shape, F32))

        def sem(name):
            return ctx.enter_context(nc.semaphore(name))

        q_all = nc.dram_tensor("q_all", (D, TERMS, T), BF16).ap()
        k_all = nc.dram_tensor("k_all", (D, TERMS, T), BF16).ap()
        q_quad, k_quad = (x.rearrange("(g a h d) r t -> g h (d r) a t", g=QUADS, a=2, h=2) for x in (q_all, k_all))

        W = sb("W", [P, PACK_W])
        R = sb("R", [P, len(ROWV), D])
        X = sb("X", [P, NT, D])
        XB = sb("XB", [P, NT, D])
        XT = sb("XT", [P, T])
        ident16 = sb("ident16", [P, P], BF16)
        mask_ts = sb("mask_ts", [P, P], BF16)
        Qn = sb("Qn", [P, 2, 3 * CH], BF16)
        Kn = sb("Kn", [P, 2, 2, 3 * CH], BF16)
        Qr = sb("Qr", [P, 2, CH], BF16)
        Kr = sb("Kr", [P, 2, 2, T], BF16)
        V = sb("V", [P, NT, H, HD])
        Vq = sb("Vq", [P, NT, 4, 32])
        work = sb("work", [P, 8 * 1024])
        probs = work[:, :].rearrange("p (s j n) -> p s j n", s=SLOTS, j=4)
        hid = work[:, :].rearrange("p (s k n) -> p s k n", s=4, k=KH)
        O = sb("O", [P, QUADS, T])
        flat = O[:, :, :].rearrange("p g t -> p (g t)")
        uq, uk, rq, rk = (flat[:, 2 * k * CH:2 * (k + 1) * CH].rearrange("p (s n) -> p s n", s=2) for k in (0, 1, 3, 4))
        tq, tk = flat[:, 4 * CH:5 * CH], flat[:, 5 * CH:6 * CH]
        angles = work[:, 2 * T:4 * T].rearrange("p (f n) -> p f n", f=2)
        parts16 = flat[:, 10 * CH:16 * CH].bitcast(BF16).rearrange("p (s k n) -> p s k n", s=4, k=3)
        q_parts = [parts16[:, s] for s in (0, 1)]
        k_parts = [parts16[:, s] for s in (2, 3)]
        maxp = sb("maxp", [P, 2, 16, NC])
        mx = sb("mx", [P, 2, 16])
        mres = sb("mres", [P, 2, 16])
        nmax = sb("nmax", [P, 2, 16, 3], BF16)
        mrow = sb("mrow", [12, 2, CH], BF16)
        rden = sb("rden", [P, 2, H])
        attn = sb("attn", [P, 2, D])
        attnT = sb("attnT", [P, 2, D])
        Y = sb("Y", [P, 2, TPC, D])
        stats = sb("stats", [P, 2, TPC, 6])
        mean_var = sb("mean_var", [P, 2, TPC, 2])
        veps = sb("veps", [P, 2, TPC])
        rstd = sb("rstd", [P, 2, TPC])
        mhalf = sb("mhalf", [P, TPC])
        waited = sb("waited", [P, TPC])

        ST = psum("ST", [P, RING, 512])
        MX = psum("MX", [P, RING, 512])
        OT = psum("OT", [P, 512])
        MT = psum("MT", [P, 512])
        bank_of = [ST[:, 0, :], ST[:, 1, :], ST[:, 2, :], MX[:, 0, :], MX[:, 1, :], MX[:, 2, :], OT[:, :], MT[:, :]]
        half = [ST[:, 0, :], ST[:, 1, :], ST[:, 2, :], MX[:, 2, :]]

        def q_banks(L, c):
            return (half[2], None) if L else (bank_of[5 * c % 8], bank_of[(5 * c + 1) % 8])

        def k_banks(L, c):
            return (half[1], None) if L else (bank_of[(5 * c + 2) % 8], bank_of[(5 * c + 3) % 8])

        def v_bank(L, c):
            return MT[:, :] if L else bank_of[(5 * c + 4) % 8]

        def w(name, k=0, n=None):
            at, width = OFF[name]
            n = width if n is None else n
            return W[:, at + k * n:at + (k + 1) * n]

        def row(name):
            return R[:, ROWV.index(name), :]

        s_w1 = sem("s_w1")
        s_xin = sem("s_xin")
        s_masks = sem("s_masks")
        s_rest = sem("s_rest")
        s_rows = sem("s_rows")
        s_x = sem("s_x")
        s_ang = [sem("s_ang0"), sem("s_ang1")]
        s_cst = sem("s_cst")
        s_c16 = sem("s_c16")
        s_proj = sem("s_proj")
        s_took = sem("s_took")
        s_rot = sem("s_rot")
        s_uq, s_uk = sem("s_uq"), sem("s_uk")
        s_q1, s_k1 = sem("s_q1"), sem("s_k1")
        s_rq, s_rk = sem("s_rq"), sem("s_rk")
        s_q2, s_k2 = sem("s_q2"), sem("s_k2")
        s_q3, s_k3 = sem("s_q3"), sem("s_k3")
        s_qst = [sem("s_qst0"), sem("s_qst1")]
        s_kst = [sem("s_kst0"), sem("s_kst1")]
        s_n = [sem(f"s_n{k}") for k in range(NC - 1)]
        s_kr = [sem(f"s_kr{k}") for k in range(NC)]
        s_qr = sem("s_qr")
        s_vq = sem("s_vq")
        s_max = sem("s_max")
        s_red = sem("s_red")
        s_comb = sem("s_comb")
        s_nmax = sem("s_nmax")
        s_mtp = sem("s_mtp")
        s_mrow = sem("s_mrow")
        s_mq = [sem("s_mq0"), sem("s_mq1")]
        s_st = sem("s_st")
        s_exp = sem("s_exp")
        s_tri = sem("s_tri")
        s_pv = sem("s_pv")
        s_oe = sem("s_oe")
        s_turn = sem("s_turn")
        s_rden = sem("s_rden")
        s_attn = sem("s_attn")
        s_atp = sem("s_atp")
        s_ate = sem("s_ate")
        s_wo = sem("s_wo")
        s_y = sem("s_y")
        s_yr = sem("s_yr")
        s_t3 = sem("s_t3")
        s_bn = sem("s_bn")
        s_mv = sem("s_mv")
        s_ve = sem("s_ve")
        s_rs = sem("s_rs")
        s_ln = sem("s_ln")
        s_xb = sem("s_xb")
        s_xtp = sem("s_xtp")
        s_xt = sem("s_xt")
        s_ha = sem("s_ha")
        s_hr = sem("s_hr")
        s_hb = sem("s_hb")
        s_hm = sem("s_hm")
        s_out = sem("s_out")

        block = ctx.enter_context(nc.Block())

        def q_src(c):
            return (Qn, c * CH) if c < NC - 1 else (Qr, 0)

        @block.sync
        def _(sp):
            sp.dma_start(W[:, 0:FIRST_END], pack[:, 0:FIRST_END]).then_inc(s_w1, 16)
            sp.dma_start(XT[:, 0:CH], xT_in[:, 0:CH]).then_inc(s_w1, 16)
            sp.dma_start(XT[:, CH:T], xT_in[:, CH:T]).then_inc(s_xin, 16)
            def store_parts(L, c):
                n = NC * L + c
                for done, parts, dst, landed in ((s_q3, q_parts, q_all, s_qst), (s_k3, k_parts, k_all, s_kst)):
                    sp.wait_ge(done, n + 1)
                    for term, terms, q_part, k_part in RUNS:
                        if dst is q_all:
                            src = parts[n % 2][:, q_part:q_part + 1, :].to_broadcast([P, terms, CH])
                        else:
                            src = parts[n % 2][:, k_part:k_part + terms, :]
                        sp.dma_start(dst[:, term:term + terms, c * CH:(c + 1) * CH], src).then_inc(landed[n % 2], 16)

            def stored(L, c):
                for landed in (s_qst[c % 2], s_kst[c % 2]):
                    sp.wait_ge(landed, 16 * len(RUNS) * (NC // 2 * L + c // 2 + 1))

            def load(dst, quad, g, h, k, landed):
                sp.dma_start(dst, quad[bass.ds(g, 1), h, :, :, k * CH:(k + 1) * CH].rearrange("g p a t -> (g p) a t"))\
                  .then_inc(landed, 16)

            def load_keys(K, g, k, landed):
                for h in range(2):
                    load(K[ROWS * h:ROWS * h + MROW, :, h, k * CH:(k + 1) * CH], k_quad, g, h, k, landed)

            def load_near(g, k):
                for h in range(2):
                    load(Qn[ROWS * h:ROWS * h + MROW, :, k * CH:(k + 1) * CH], q_quad, g, h, k, s_n[k])
                load_keys(Kn, g, k, s_n[k])

            def load_last_queries(g):
                for h in range(2):
                    load(Qr[ROWS * h:ROWS * h + MROW, :, :], q_quad, g, h, NC - 1, s_qr)

            def place_max(L, g, c):
                G = QUADS * L + g
                sp.wait_ge(s_mrow, NC * G + c + 1)
                dst, at = q_src(c)
                for j in range(4):
                    p0 = ROWS * (j % 2) + MROW
                    sp.dma_start(dst[p0:p0 + 3, j // 2, at:at + CH], mrow[3 * j:3 * j + 3, c % 2, :])\
                      .then_inc(s_mq[c % 2], 16)

            def passed(L, g, u):
                sp.wait_ge(s_st, 4 * (NSTEP * (QUADS * L + g) + u))

            def back(L, g, more):
                if more:
                    passed(L, g, STEP0[2] + TPC)
                    load_near(g + 1, 0)
                    passed(L, g, STEP0[2] + 2 * TPC)
                    load_near(g + 1, 1)
                place_max(L, g, 3)
                if more:
                    passed(L, g, STEP0[3])
                    load_near(g + 1, 2)
                    place_max(L, g + 1, 0)
                    place_max(L, g + 1, 1)
                    for k in range(NC - 1):
                        passed(L, g, STEP0[3] + TPC * (k + 1))
                        load_keys(Kr, g + 1, k, s_kr[k])
                    passed(L, g, NSTEP)
                    load_last_queries(g + 1)
                    load_keys(Kr, g + 1, 3, s_kr[3])

            for L in range(2):
                for k in range(NC - 1):
                    store_parts(L, k)
                    if L == 0 and k == 0:
                        sp.wait_ge(s_c16, 2)
                        sp.wait_ge(s_cst, 7)
                    stored(L, k)
                    load_near(0, k)
                store_parts(L, NC - 1)
                place_max(L, 0, 0)
                if L == 0:
                    sp.wait_ge(s_cst, 11)
                for k in range(NC - 1):
                    load_keys(Kr, 0, k, s_kr[k])
                stored(L, NC - 1)
                load_keys(Kr, 0, NC - 1, s_kr[NC - 1])
                load_last_queries(0)
                place_max(L, 0, 1)
                place_max(L, 0, 2)
                with sp.Fori(0, QUADS - 1) as g:
                    back(L, g, True)
                    place_max(L, g + 1, 2)
                back(L, QUADS - 1, False)
            o_view = out[0].rearrange("(n p) d -> p n d", p=P)
            for c in range(NC):
                sp.wait_ge(s_ln, 3 * NC + c + 1)
                sp.dma_start(o_view[:, TPC * c:TPC * (c + 1), :], X[:, TPC * c:TPC * (c + 1), :]).then_inc(s_out, 16)
            sp.wait_ge(s_out, 16 * NC)

        @block.gpsimd
        def _(pool):
            pool.memset(Qn[:, :, :], 0.0).then_inc(s_cst, 1)
            pool.memset(Qr[:, :, :], 0.0).then_inc(s_cst, 1)
            pool.memset(mhalf[:, :], -0.5).then_inc(s_cst, 1)
            pool.memset(Vq[:, :, :, :], 0.0).then_inc(s_cst, 1)
            pool.wait_ge(s_cst, 4)
            pool.memset(Vq[:, :, :, HD:HD + 1], 1.0).then_inc(s_cst, 1)

            for h in range(2):
                pool.wait_ge(s_cst, 5 + h)
                pool.memset(Kn[ROWS * h + ROWS // 2:ROWS * (h + 1), :, h, :], 1.0).then_inc(s_cst, 1)
            pool.wait_ge(s_cst, 7)

            def rest_of_keys(h, part):
                p0, rows, value = ((ROWS * (1 - h), ROWS, 0.0), (ROWS * h + ROWS // 2, ROWS // 2, 1.0))[part]
                pool.wait_ge(s_cst, 7 + 2 * h + part)
                pool.memset(Kr[p0:p0 + rows, :, h, :], value).then_inc(s_cst, 1)

            def add_bias(phase, name, c):
                if phase:
                    pool.wait_ge(s_ln, NC * (phase - 1) + c + 1)
                elif c == 0:
                    pool.wait_ge(s_x, 16)
                    pool.wait_ge(s_rows, 16)
                pool.tensor_tensor(XB[:, TPC * c:TPC * (c + 1), :], X[:, TPC * c:TPC * (c + 1), :],
                                   row(name).unsqueeze(1).to_broadcast([P, TPC, D]), ALU.add).then_inc(s_xb, 1)

            def split_keys(L, c):
                n = NC * L + c
                if L == 0:
                    pool.wait_ge(s_k1, n + 1)
                    pool.wait_ge(s_uk, n + 1)
                    pool.tensor_tensor(rk[:, n % 2], uk[:, n % 2], k_parts[n % 2][:, 0, :], ALU.subtract)\
                        .then_inc(s_rk, 1)
                pool.wait_ge(s_k2, n + 1)
                pool.wait_ge(s_rk, n + 1)
                pool.tensor_tensor(k_parts[n % 2][:, 2, :], rk[:, n % 2], k_parts[n % 2][:, 1, :], ALU.subtract)\
                    .then_inc(s_k3, 1)

            def take_values(L, g, k):
                pool.tensor_copy(Vq[:, TPC * k:TPC * (k + 1), :, 0:HD],
                                 V[:, TPC * k:TPC * (k + 1), bass.ds(4 * g, 4), :]).then_inc(s_vq, 1)

            def clear_early(L, g, u):
                G = QUADS * L + g
                if not (L == 0 and isinstance(g, int) and g == 0 and u == DIAG[0]):
                    pool.wait_ge(s_tri, len(DIAG) * G + DIAG.index(u))
                pool.wait_ge(s_exp, 4 * (NSTEP * G + u + 1))
                pool.tensor_tensor(waited[:, :], mhalf[:, :], mhalf[:, :], ALU.add)
                for _, _, col in STEPS[u][1]:
                    p = probs[:, u % SLOTS, :, col:col + P]
                    ins = pool.affine_select(out=p, in_=p, compare_op=ALU.is_ge, fill=0.0, base=0,
                                             pattern=[[0, 4], [1, P]], channel_multiplier=-1)
                ins.then_inc(s_tri, 1)

            def next_values(L, g, k):
                pool.wait_ge(s_pv, NSTEP * (QUADS * L + g) + (STEP0[3] + TPC * (k + 1) if k < 3 else NSTEP))
                take_values(L, g + 1, k)

            def attention(L, bias):
                clear_early(L, 0, DIAG[0])
                clear_early(L, 0, DIAG[1])
                with pool.Fori(0, QUADS - 1) as g:
                    for u in DIAG[2:9]:
                        clear_early(L, g, u)
                    next_values(L, g, 0)
                    next_values(L, g, 1)
                    clear_early(L, g, DIAG[9])
                    next_values(L, g, 2)
                    clear_early(L, g, DIAG[10])
                    clear_early(L, g, DIAG[11])
                    clear_early(L, g + 1, DIAG[0])
                    next_values(L, g, 3)
                    clear_early(L, g + 1, DIAG[1])
                g = QUADS - 1
                for u in DIAG[2:6]:
                    clear_early(L, g, u)
                for c in range(NC):
                    add_bias(2 * L, bias, c)
                for u in DIAG[6:9]:
                    clear_early(L, g, u)
                for c in range(2):
                    powers(2 * L, c)
                    if L == 0:
                        add_bias(1, "b2", c)
                for u in DIAG[9:]:
                    clear_early(L, g, u)
                for c in range(2, NC):
                    powers(2 * L, c)
                    if L == 0:
                        add_bias(1, "b2", c)

            def powers(phase, c):
                n = NC * phase + c
                pool.wait_ge(s_mv, n + 1)
                pool.tensor_scalar(veps[:, n % 2, :], mean_var[:, n % 2, :, 1], EPS, None, ALU.add).then_inc(s_ve, 1)
                pool.wait_ge(s_ve, n + 1)
                pool.tensor_tensor(rstd[:, n % 2, :], veps[:, n % 2, :], mhalf[:, :], ALU.pow).then_inc(s_rs, 1)

            def first_values(L):
                for k in range(NC):
                    pool.wait_ge(s_took, NC * L + k + 1)
                    take_values(L, 0, k)

            for c in range(NC):
                split_keys(0, c)
                pool.wait_ge(s_k3, c + 1)
                rest_of_keys(*divmod(c, 2))
                pool.wait_ge(s_cst, 8 + c)
            first_values(0)
            attention(0, "bo")
            for step in range(NC + 2):
                if step < NC:
                    powers(1, step)
                if step >= 2:
                    split_keys(1, step - 2)
            first_values(1)
            attention(1, "bo1")
            for c in range(NC):
                powers(3, c)

        @block.tensor
        def _(pe):
            def project(L, c):
                n = NC * L + c
                xt = XT[:, c * CH:(c + 1) * CH]
                if L:
                    pe.wait_ge(s_xt, NC + c + 1)
                    pe.wait_ge(s_rq, n)
                elif c == 0:
                    pe.wait_ge(s_w1, 32)
                else:
                    if c == 1:
                        pe.wait_ge(s_xin, 16)
                    if c >= 2:
                        pe.wait_ge(s_uk, c - 1)
                plain, swapped = q_banks(L, c)
                mm = pe.matmul(plain, w("Wq1" if L else "Wq"), xt, start=True, stop=True)
                if L == 0:
                    mm = pe.matmul(swapped, w("Wqs"), xt, start=True, stop=True)
                mm.then_inc(s_proj, 1)
                if L:
                    pe.wait_ge(s_rk, n)
                    if c == 0:
                        pe.wait_ge(s_hr, KH * NC)
                elif c:
                    pe.wait_ge(s_uq, c)
                plain, swapped = k_banks(L, c)
                mm = pe.matmul(plain, w("Wk1" if L else "Wk"), xt, start=True, stop=True)
                if L == 0:
                    mm = pe.matmul(swapped, w("Wks"), xt, start=True, stop=True)
                mm.then_inc(s_proj, 1)
                if L:
                    pe.wait_ge(s_took, n)
                    if c == 0:
                        pe.wait_ge(s_yr, NC)
                for i in range(TPC):
                    mm = pe.matmul(v_bank(L, c)[:, i * P:(i + 1) * P], XT[:, c * CH + i * P:c * CH + (i + 1) * P],
                                   w("Wv1" if L else "Wv"), start=True, stop=True)
                mm.then_inc(s_proj, 1)

            def max_block(L, g, b):
                n = NMAX * (QUADS * L + g) + b
                c, i, j0, heads, k, width = BLOCKS[b]
                Q, at = q_src(c)
                K = Kr if c == NC - 1 else Kn
                if b == 0 or BLOCKS[b - 1][0] != c:
                    if c == NC - 1:
                        pe.wait_ge(s_qr, 32 * (QUADS * L + g + 1))
                    else:
                        pe.wait_ge(s_n[c], 64 * (QUADS * L + g + 1))
                if c == NC - 1 and BLOCKS[b - 1][4] != k or b == MAX_END[2]:
                    pe.wait_ge(s_kr[k], 32 * (QUADS * L + g + 1))
                if not (L == 0 and isinstance(g, int) and g == 0 and b < RING):
                    pe.wait_ge(s_red, n - 2 if b >= RING - 1 else n - 1)
                for h in range(heads):
                    j = j0 + h
                    dst = MX[:, b % RING, h * width:(h + 1) * width]
                    mm = pe.matmul(dst, Q[:, j // 2, at + i * P:at + (i + 1) * P],
                                   K[:, j // 2, j % 2, k * CH:k * CH + width], start=True, stop=k < c)
                    if k == c:
                        mm = pe.matmul(dst[:, i * P:(i + 1) * P], ident16[:, :], mask_ts[:, :], start=False, stop=True)
                mm.then_inc(s_max, 1)

            def max_rows(L, g, c):
                n = NC * (QUADS * L + g) + c
                pe.wait_ge(s_nmax, n + 1)
                pe.wait_ge(s_mrow, n)
                for i in range(TPC):
                    mm = pe.matmul(MT[0:12, i * P:(i + 1) * P],
                                   nmax[:, c % 2, 4 * i:4 * i + 4, :].rearrange("p j k -> p (j k)"), ident16[:, :],
                                   start=True, stop=True)
                mm.then_inc(s_mtp, 1)

            def scores(L, g, u, j):
                G = QUADS * L + g
                idx = 4 * (NSTEP * G + u) + j
                c, tiles = STEPS[u]
                Q, at = q_src(c)
                K = Kr if c == NC - 1 else Kn
                if u == STEP0[c] and j == 0:
                    pe.wait_ge(s_mq[c % 2], 64 * (2 * G + c // 2 + 1))
                if not (L == 0 and isinstance(g, int) and g == 0 and 4 * u + j < RING):
                    pe.wait_ge(s_exp, idx - 2)
                bank = ST[:, (4 * u + j) % RING, :]
                for tile, t0, col in tiles:
                    mm = pe.matmul(bank[:, col:col + CH - t0], K[:, j // 2, j % 2, tile * P:(tile + 1) * P],
                                   Q[:, j // 2, at + t0:at + CH], start=True, stop=True)
                mm.then_inc(s_st, 1)

            def sums(L, g, u, new):
                G = QUADS * L + g
                c, tiles = STEPS[u]
                if u == STEP0[c]:
                    if not (new and c == 0):
                        pe.wait_ge(s_oe, NC * G + c)
                    pe.wait_ge(s_vq, NC * G + c + 1)
                if u in DIAG:
                    pe.wait_ge(s_tri, len(DIAG) * G + DIAG.index(u) + 1)
                else:
                    pe.wait_ge(s_exp, 4 * (NSTEP * G + u + 1))
                for tile, t0, col in tiles:
                    for j in range(4):
                        mm = pe.matmul(OT[32 * j:32 * j + 32, t0:CH], Vq[:, tile, j, :],
                                       probs[:, u % SLOTS, j, col:col + CH - t0], start=(tile == 0),
                                       stop=(u in LAST and tile == tiles[-1][0]), skip_group_check=True)
                mm.then_inc(s_pv, 1)

            def step(L, g, u, more, new):
                done = START_DONE if new else DONE
                rows_at = START_ROWS_AT if new else ROWS_AT
                first = 0 if u == TURN else done[u]
                count = done[u + 1] - first
                ahead = 1 if u >= TURN else 0

                def max_blocks(part):
                    if more or not ahead:
                        for b in range(first + count * part // 4, first + count * (part + 1) // 4):
                            max_block(L, g + ahead, b)

                scores(L, g, u, 0)
                max_blocks(0)
                scores(L, g, u, 1)
                max_blocks(1)
                if u >= LAG:
                    sums(L, g, u - LAG, new)
                elif not new:
                    sums(L, g - 1, NSTEP + u - LAG, False)
                max_blocks(2)
                if u in rows_at and (more or not rows_at[u][0]):
                    max_rows(L, g + rows_at[u][0], rows_at[u][1])
                scores(L, g, u, 2)
                max_blocks(3)
                if not more and u >= OUT_STEP:
                    out_stages(L, u - OUT_STEP, EARLY)
                scores(L, g, u, 3)

            def steps(L, g, first, end, more=True, new=False):
                for u in range(first, end):
                    step(L, g, u, more, new)

            def attention(L):
                for b in range(MAX_END[0] if L else 0, START_DONE[0]):
                    max_block(L, 0, b)
                    if b == MAX_END[0] + RING - 1:
                        max_rows(L, 0, 0)
                steps(L, 0, 0, CUT, new=True)
                with pe.Fori(0, QUADS - 1) as g:
                    steps(L, g, CUT, NSTEP)
                    steps(L, g + 1, 0, CUT)
                steps(L, QUADS - 1, CUT, NSTEP, more=False)
                for u in range(NSTEP - LAG, NSTEP):
                    sums(L, QUADS - 1, u, False)

            def turn_sums(L, tile):
                n = NT * L + tile
                if tile == 0:
                    pe.wait_ge(s_red, NMAX * QUADS * (L + 1))
                if tile % TPC == 0:
                    pe.wait_ge(s_oe, NC * (QUADS * L + QUADS - 1) + tile // TPC + 1)
                if n >= 2:
                    pe.wait_ge(s_attn, n - 1)
                for g in range(QUADS):
                    mm = pe.transpose(MX[:, n % 2, g * P:(g + 1) * P], O[:, g, tile * P:(tile + 1) * P], w("ident"))
                mm.then_inc(s_turn, 1)

            def turn_attention(L, tile):
                n = NT * L + tile
                pe.wait_ge(s_attn, n + 1)
                if n:
                    pe.wait_ge(s_ate, n)
                pe.transpose(MX[:, 2, 0:P], attn[:, n % 2, :], w("ident")).then_inc(s_atp, 1)

            def output_product(L, tile):
                n = NT * L + tile
                c, i = divmod(tile, TPC)
                ln = 2 * NC * L + c
                pe.wait_ge(s_ate, n + 1)
                if n == 0:
                    pe.wait_ge(s_rest, 16)
                if tile == 0:
                    pe.wait_ge(s_mrow, NC * QUADS * (L + 1))
                if i == 0 and ln:
                    pe.wait_ge(s_yr, ln)
                pe.matmul(MT[:, i * P:(i + 1) * P], attnT[:, n % 2, :], w("Wo1" if L else "Wo"),
                          start=True, stop=True).then_inc(s_wo, 1)

            def out_stages(L, tile, end, first=0):
                for stage, t in ((turn_sums, tile), (turn_attention, tile - 1), (output_product, tile - 2)):
                    if first <= t < end:
                        stage(L, t)

            def last_tiles(L):
                for tile in range(EARLY, NT + 2):
                    out_stages(L, tile, NT, EARLY)
                    if tile == EARLY:
                        pe.wait_ge(s_exp, 4 * NSTEP * QUADS * (L + 1))
                    if tile - EARLY < NC - 1:
                        channels(2 * NC * L + tile - EARLY)

            def channels(ln):
                pe.wait_ge(s_ln, ln + 1)
                pe.wait_ge(s_xt, ln)
                c = ln % NC
                for i in range(TPC):
                    mm = pe.transpose(OT[:, i * P:(i + 1) * P], X[:, TPC * c + i, :], w("ident"))
                mm.then_inc(s_xtp, 1)

            def out_product(ln, slot, weight):
                c = ln % NC
                pe.wait_ge(s_yr, ln - 1)
                for i in range(TPC):
                    for k in range(KH):
                        mm = pe.matmul(MX[:, c % 2, i * P:(i + 1) * P], hid[:, slot, k, i * P:(i + 1) * P],
                                       w(weight, k, D), start=(k == 0), stop=(k == KH - 1))
                mm.then_inc(s_y, 1)

            def mlp0_and_project():
                pe.wait_ge(s_ate, NT)
                for step in range(NC + 3):
                    if step < NC:
                        pe.wait_ge(s_xt, step + 1)
                        for m in range(KH):
                            n = KH * step + m
                            if n >= 2:
                                pe.wait_ge(s_hr, n - 1)
                            pe.matmul(half[n % 2], w("W1", m, P), XT[:, step * CH:(step + 1) * CH],
                                      start=True, stop=True).then_inc(s_ha, 1)
                    if step == 1:
                        channels(NC - 1)
                    if 1 <= step <= NC:
                        pe.wait_ge(s_hr, KH * step)
                        out_product(NC + step - 1, step - 1, "W2")
                    if 2 <= step <= NC + 1:
                        channels(NC + step - 2)
                    if step >= 3:
                        project(1, step - 3)
                    if step == NC + 1:
                        pe.wait_ge(s_yr, 2 * NC)
                        for b in range(MAX_END[0]):
                            max_block(1, 0, b)

            def mlp1():
                pe.wait_ge(s_ate, 2 * NT)
                for kind, c in MLP1:
                    if kind == "out":
                        pe.wait_ge(s_hr, mlp1_index("h2", c) + KH)
                        out_product(3 * NC + c, c % 2, "W3")
                        continue
                    if kind == "turn":
                        channels(2 * NC + c)
                        continue
                    at = mlp1_index(kind, c)
                    if kind == "gate":
                        pe.wait_ge(s_xt, 2 * NC + c + 1)
                    elif kind == "h1":
                        pe.wait_ge(s_hm, KH * (c + 1))
                    else:
                        pe.wait_ge(s_hr, mlp1_index("h1", c) + KH)
                    for m in range(KH):
                        n = at + m
                        pe.wait_ge(s_hr, n - 1)
                        if kind == "gate":
                            pe.matmul(half[n % 2], w("A", m, P), XT[:, c * CH:(c + 1) * CH], start=True, stop=True)\
                              .then_inc(s_ha, 1)
                            b = KH * c + m
                            if b >= 2:
                                pe.wait_ge(s_hm, b - 1)
                            pe.matmul(half[2 + b % 2], w("B", m, P), XT[:, c * CH:(c + 1) * CH], start=True, stop=True)\
                              .then_inc(s_hb, 1)
                        else:
                            slot = c % 2 if kind == "h1" else 2 + c % 2
                            weight = "H1" if kind == "h1" else "H2"
                            for k in range(KH):
                                mm = pe.matmul(half[n % 2], w(weight, k, HID)[:, m * P:(m + 1) * P], hid[:, slot, k, :],
                                               start=(k == 0), stop=(k == KH - 1))
                            mm.then_inc(s_ha, 1)

            for c in range(NC):
                project(0, c)
            pe.wait_ge(s_c16, 4)
            for L in range(2):
                pe.wait_ge(s_rk if L else s_uk, NC * (L + 1))
                pe.wait_ge(s_took, NC * (L + 1))
                attention(L)
                last_tiles(L)
                (mlp1 if L else mlp0_and_project)()

        @block.scalar
        def _(act):
            def split(L, c):
                n = NC * L + c
                which = ((uq, rq, q_parts, s_uq, s_rq, s_q1, s_q2, s_qst, SCALE),
                         (uk, rk, k_parts, s_uk, s_rk, s_k1, s_k2, s_kst, 1.0))
                for i, (u, _, parts, ready, _, one, _, landed, scale) in enumerate(which):
                    if L:
                        act.wait_ge(s_proj, 3 * n + i + 1)
                        src = (q_banks(L, c), k_banks(L, c))[i][0]
                    else:
                        act.wait_ge(ready, n + 1)
                        src = u[:, n % 2]
                    if n >= 2:
                        act.wait_ge(landed[n % 2], 16 * len(RUNS) * (n // 2))
                    act.activation(parts[n % 2][:, 0, :], src, ACT.Copy, scale=scale).then_inc(one, 1)
                if L:
                    act.wait_ge(s_proj, 3 * n + 3)
                    act.activation(V[:, TPC * c:TPC * (c + 1), :, :].rearrange("p n h d -> p (n h d)"), v_bank(L, c),
                                   ACT.Copy).then_inc(s_took, 1)
                for _, r, parts, _, rest, _, two, _, _ in which:
                    act.wait_ge(rest, n + 1)
                    act.activation(parts[n % 2][:, 1, :], r[:, n % 2], ACT.Copy).then_inc(two, 1)

            def keep_rows(L, g, c):
                n = NC * (QUADS * L + g) + c
                act.wait_ge(s_mtp, n + 1)
                act.activation(mrow[:, c % 2, :], MT[0:12, :], ACT.Copy).then_inc(s_mrow, 1)

            def keep_sums(L, g, c):
                act.wait_ge(s_pv, NSTEP * (QUADS * L + g) + LAST[c] + 1)
                act.activation(O[:, bass.ds(g, 1), c * CH:(c + 1) * CH].rearrange("p g t -> p (g t)"), OT[:, :],
                               ACT.Copy).then_inc(s_oe, 1)

            def steps(L, g, first, end, more=True, new=False):
                G = QUADS * L + g
                rows_at = START_ROWS_AT if new else ROWS_AT
                for u in range(first, end):
                    c = STEPS[u][0]
                    for j in range(4):
                        if j == 2 and u == STEP0[c] + LAG - 1 and not (new and c == 0):
                            keep_sums(L, *((g, c - 1) if c else (g - 1, NC - 1)))
                        if j == 3 and u in rows_at and (more or not rows_at[u][0]):
                            keep_rows(L, g + rows_at[u][0], rows_at[u][1])
                        if j == 3 and not more and 0 <= u - OUT_STEP - 1 < EARLY:
                            keep_attention(L, u - OUT_STEP - 1)
                        act.wait_ge(s_st, 4 * (NSTEP * G + u) + j + 1)
                        if not (new and u < SLOTS):
                            act.wait_ge(s_pv, NSTEP * G + u - SLOTS + 1)
                        act.activation(probs[:, u % SLOTS, j, 0:WIDTH[u]], ST[:, (4 * u + j) % RING, 0:WIDTH[u]],
                                       ACT.Exp).then_inc(s_exp, 1)

            def keep_channels(ln):
                act.wait_ge(s_xtp, ln + 1)
                c = ln % NC
                act.activation(XT[:, c * CH:(c + 1) * CH], OT[:, :], ACT.Copy).then_inc(s_xt, 1)

            def keep_attention(L, tile):
                n = NT * L + tile
                act.wait_ge(s_atp, n + 1)
                if n >= 2:
                    act.wait_ge(s_wo, n - 1)
                act.activation(attnT[:, n % 2, :], MX[:, 2, 0:P], ACT.Copy).then_inc(s_ate, 1)

            def last_tiles(L):
                for tile in range(EARLY, NT):
                    if tile - EARLY < NC - 1:
                        keep_channels(2 * NC * L + tile - EARLY)
                    keep_attention(L, tile)

            def mlp0_and_split():
                for step in range(NC + 3):
                    if step < NC:
                        for m in range(KH):
                            n = KH * step + m
                            act.wait_ge(s_ha, n + 1)
                            act.activation(hid[:, step, m, :], half[n % 2], ACT.Gelu,
                                           bias=w("b1", m, 1)).then_inc(s_hr, 1)
                    if step == 1:
                        keep_channels(NC - 1)
                    if 2 <= step <= NC + 1:
                        keep_channels(NC + step - 2)
                    if step >= 3:
                        split(1, step - 3)

            def mlp1():
                for kind, c in MLP1:
                    if kind == "out":
                        continue
                    if kind == "turn":
                        keep_channels(2 * NC + c)
                        continue
                    at = mlp1_index(kind, c)
                    if kind == "gate" and c >= 2:
                        act.wait_ge(s_y, NC + c - 1)
                    for m in range(KH):
                        n = at + m
                        act.wait_ge(s_ha, n + 1)
                        if kind == "gate":
                            act.activation(hid[:, c % 2, m, :], half[n % 2], ACT.Silu,
                                           scale=w("sa", m, 1)).then_inc(s_hr, 1)
                        elif kind == "h1":
                            act.activation(hid[:, 2 + c % 2, m, :], half[n % 2], ACT.Gelu,
                                           scale=w("s1", m, 1)).then_inc(s_hr, 1)
                        else:
                            act.activation(hid[:, c % 2, m, :], half[n % 2], ACT.Gelu,
                                           scale=w("s2", m, 1)).then_inc(s_hr, 1)

            for f, table in enumerate((cos, sin)):
                act.dma_start(angles[:, f, 0:CH], table[:, 0:CH]).then_inc(s_ang[0], 16)
            act.dma_start(R[:, :, :].rearrange("p a b -> p (a b)"), rows.partition_broadcast(P)).then_inc(s_rows, 16)
            for f, table in enumerate((cos, sin)):
                act.dma_start(angles[:, f, CH:T], table[:, CH:T]).then_inc(s_ang[1], 16)
            act.dma_start(W[:, FIRST_END:MASKS_END], pack[:, FIRST_END:MASKS_END]).then_inc(s_masks, 16)
            for c in range(NC):
                split(0, c)
            for L in range(2):
                keep_rows(L, 0, 0)
                steps(L, 0, 0, STEP0[1], new=True)
                if L == 0:
                    act.dma_start(X[:, :, :], x_in[0].rearrange("(n p) d -> p n d", p=P)).then_inc(s_x, 16)
                    act.dma_start(W[:, MASKS_END:], pack[:, MASKS_END:]).then_inc(s_rest, 16)
                steps(L, 0, STEP0[1], CUT, new=True)
                with act.Fori(0, QUADS - 1) as g:
                    steps(L, g, CUT, NSTEP)
                    steps(L, g + 1, 0, CUT)
                steps(L, QUADS - 1, CUT, NSTEP, more=False)
                keep_sums(L, QUADS - 1, NC - 1)
                last_tiles(L)
                (mlp1 if L else mlp0_and_split)()

        @block.vector
        def _(dve):
            def project0(c):
                n = c
                if c < 2:
                    dve.wait_ge(s_ang[c], 32)
                for qk, (u, t, ready, name, banks) in enumerate(((uq, tq, s_uq, "bq", q_banks(0, c)),
                                                                 (uk, tk, s_uk, "bk", k_banks(0, c)))):
                    u = u[:, n % 2]
                    dve.wait_ge(s_proj, 3 * n + qk + 1)
                    if n >= 2:
                        dve.wait_ge(s_k3 if qk else s_q3, n - 1)
                    dve.scalar_tensor_tensor(u, banks[0], w(name), angles[:, 0, c * CH:(c + 1) * CH], ALU.add, ALU.mult)
                    dve.scalar_tensor_tensor(t, banks[1], w(name + "s"), angles[:, 1, c * CH:(c + 1) * CH], ALU.add,
                                             ALU.mult).then_inc(s_rot, 1)
                    dve.wait_ge(s_rot, 2 * n + qk + 1)
                    dve.tensor_tensor(u, u, t, ALU.add).then_inc(ready, 1)
                dve.wait_ge(s_proj, 3 * n + 3)
                if c == 0:
                    dve.wait_ge(s_rows, 16)
                dve.tensor_tensor(V[:, TPC * c:TPC * (c + 1), :, :].rearrange("p n h d -> p n (h d)"),
                                  v_bank(0, c).rearrange("p (n e) -> p n e", n=TPC),
                                  row("bv").unsqueeze(1).to_broadcast([P, TPC, D]), ALU.add).then_inc(s_took, 1)
                if c:
                    third_part(0, c - 1)
                dve.wait_ge(s_q1, n + 1)
                dve.wait_ge(s_uq, n + 1)
                dve.scalar_tensor_tensor(rq[:, n % 2], uq[:, n % 2], SCALE, q_parts[n % 2][:, 0, :], ALU.mult,
                                         ALU.subtract).then_inc(s_rq, 1)

            def project1(c):
                n = NC + c
                dve.wait_ge(s_q1, n + 1)
                dve.wait_ge(s_q3, n - 1)
                dve.scalar_tensor_tensor(rq[:, n % 2], q_banks(1, c)[0], SCALE, q_parts[n % 2][:, 0, :], ALU.mult,
                                         ALU.subtract).then_inc(s_rq, 1)
                dve.wait_ge(s_k1, n + 1)
                dve.wait_ge(s_k3, n - 1)
                dve.tensor_tensor(rk[:, n % 2], k_banks(1, c)[0], k_parts[n % 2][:, 0, :], ALU.subtract)\
                   .then_inc(s_rk, 1)
                third_part(1, c)

            def third_part(L, c):
                n = NC * L + c
                dve.wait_ge(s_q2, n + 1)
                dve.wait_ge(s_rq, n + 1)
                dve.tensor_tensor(q_parts[n % 2][:, 2, :], rq[:, n % 2], q_parts[n % 2][:, 1, :], ALU.subtract)\
                   .then_inc(s_q3, 1)

            def max_chunk(L, g, c):
                G = QUADS * L + g
                for b in range(MAX_END[c - 1] if c else 0, MAX_END[c]):
                    _, i, j, heads, k, width = BLOCKS[b]
                    dve.wait_ge(s_max, NMAX * G + b + 1)
                    dve.reduce_max(maxp[:, c % 2, 4 * i + j:4 * i + j + heads, k],
                                   MX[:, b % RING, 0:heads * width].rearrange("p (h n) -> p h n", h=heads), AX_X)\
                       .then_inc(s_red, 1)
                n = NC * G + c
                dve.wait_ge(s_red, NMAX * G + MAX_END[c])
                dve.reduce_max(mx[:, c % 2, :], maxp[:, c % 2, :, 0:c + 1], AX_X).then_inc(s_comb, 1)
                dve.wait_ge(s_comb, 4 * n + 1)
                nm = nmax[:, c % 2, :, :]
                dve.tensor_scalar(nm[:, :, 0], mx[:, c % 2, :], -1.0, None, ALU.mult).then_inc(s_comb, 1)
                dve.wait_ge(s_comb, 4 * n + 2)
                dve.scalar_tensor_tensor(mres[:, c % 2, :], mx[:, c % 2, :], -1.0, nm[:, :, 0], ALU.mult, ALU.subtract)\
                   .then_inc(s_comb, 1)
                dve.wait_ge(s_comb, 4 * n + 3)
                dve.tensor_copy(nm[:, :, 1], mres[:, c % 2, :]).then_inc(s_comb, 1)
                dve.wait_ge(s_comb, 4 * n + 4)
                dve.tensor_tensor(nm[:, :, 2], mres[:, c % 2, :], nm[:, :, 1], ALU.subtract).then_inc(s_nmax, 1)

            def branch(ln, product_done, count):
                c = ln % NC
                y = Y[:, ln % 2, :, :]
                bank = (MX[:, c % 2, :] if ln // NC % 2 else MT[:, :]).rearrange("p (n e) -> p n e", n=TPC)
                dve.wait_ge(product_done, count)
                if ln < 3 * NC:
                    dve.wait_ge(s_xb, ln + 1)
                    dve.tensor_tensor(y, bank, XB[:, TPC * c:TPC * (c + 1), :], ALU.add).then_inc(s_yr, 1)
                else:
                    dve.tensor_tensor(y, bank, row("s3").unsqueeze(1).to_broadcast([P, TPC, D]), ALU.mult)\
                       .then_inc(s_t3, 1)
                    dve.wait_ge(s_t3, c + 1)
                    dve.tensor_tensor(y, y, X[:, TPC * c:TPC * (c + 1), :], ALU.add).then_inc(s_yr, 1)
                dve.wait_ge(s_yr, ln + 1)
                for i in range(TPC):
                    ins = dve.bn_stats(stats[:, ln % 2, i, :], Y[:, ln % 2, i, :])
                ins.then_inc(s_bn, 1)
                dve.wait_ge(s_bn, ln + 1)
                for i in range(TPC):
                    ins = dve.bn_aggr(mean_var[:, ln % 2, i, :], stats[:, ln % 2, i, :])
                ins.then_inc(s_mv, 1)

            def normalise(ln):
                c = ln % NC
                dve.wait_ge(s_rs, ln + 1)
                for i in range(TPC):
                    ins = dve.tensor_scalar(X[:, TPC * c + i, :], Y[:, ln % 2, i, :], mean_var[:, ln % 2, i, 0:1],
                                            rstd[:, ln % 2, i:i + 1], ALU.subtract, ALU.mult)
                ins.then_inc(s_ln, 1)

            def attention_out(L):
                for tile in range(NT):
                    n = NT * L + tile
                    dve.wait_ge(s_turn, n + 1)
                    bank = MX[:, n % 2, :].rearrange("p (h e) -> p h e", h=H)
                    dve.reciprocal(rden[:, n % 2, :], bank[:, :, HD]).then_inc(s_rden, 1)
                    dve.wait_ge(s_rden, n + 1)
                    if n >= 2:
                        dve.wait_ge(s_atp, n - 1)
                    dve.tensor_tensor(attn[:, n % 2, :].rearrange("p (h e) -> p h e", h=H), bank[:, :, 0:HD],
                                      rden[:, n % 2, :].unsqueeze(2).to_broadcast([P, H, HD]), ALU.mult)\
                       .then_inc(s_attn, 1)
                    for c in range(NC - 1):
                        ln = 2 * NC * L + c
                        if tile == min(TPC * c + 5, EARLY - 1):
                            branch(ln, s_wo, NT * L + TPC * (c + 1))
                        if tile == min(TPC * c + 7, EARLY - 1):
                            normalise(ln)
                branch(2 * NC * L + 3, s_wo, NT * (L + 1))
                normalise(2 * NC * L + 3)

            def mlp0_and_project():
                for step in range(1, NC + 3):
                    if step <= NC:
                        branch(NC + step - 1, s_y, step)
                    if step >= 3:
                        project1(step - 3)
                    if step == NC + 1:
                        max_chunk(1, 0, 0)
                    if step <= NC:
                        normalise(NC + step - 1)

            def mlp1():
                for kind, c in MLP1:
                    if kind == "gate":
                        for m in range(KH):
                            b = KH * c + m
                            dve.wait_ge(s_hb, b + 1)
                            dve.wait_ge(s_hr, mlp1_index("gate", c) + m + 1)
                            h = hid[:, c % 2, m, :]
                            dve.scalar_tensor_tensor(h, half[2 + b % 2], w("sb", m, 1), h, ALU.mult, ALU.mult)\
                               .then_inc(s_hm, 1)
                        if c >= 2:
                            normalise(3 * NC + c - 2)
                    if kind == "out":
                        branch(3 * NC + c, s_y, NC + c + 1)
                        if c >= 2:
                            normalise(3 * NC + c)

            for h in range(2):
                dve.memset(Kn[ROWS * (1 - h):ROWS * (2 - h), :, h, :], 0.0).then_inc(s_c16, 1)
            dve.wait_ge(s_w1, 32)
            dve.tensor_copy(ident16[:, :], w("ident")).then_inc(s_c16, 1)
            for c in range(NC):
                project0(c)
                if c == 1:
                    dve.wait_ge(s_masks, 16)
                    dve.tensor_copy(mask_ts[:, :], w("mask_ts")).then_inc(s_c16, 1)
            third_part(0, NC - 1)
            for L in range(2):
                for c in range(L, NC):
                    max_chunk(L, 0, c)
                with dve.Fori(0, QUADS - 1) as g:
                    for c in range(NC):
                        max_chunk(L, g + 1, c)
                attention_out(L)
                (mlp1 if L else mlp0_and_project)()


def kernel(**inputs):
    import numpy as np
    import concourse.bacc as bacc
    from concourse import mybir as mb
    from concourse.bass_utils import run_bass_kernel_spmd

    a = {k: np.ascontiguousarray(v) for k, v in inputs.items()}
    pair = np.arange(D) ^ 1
    spread = (np.arange(H) // 4)[:, None] * HD + np.arange(HD)[None]
    spread = spread.reshape(-1)

    def tiles(m):
        return m.reshape(-1, P, m.shape[1]).transpose(1, 0, 2).reshape(P, -1)

    def cols(v):
        return v.reshape(-1, P).T

    low = np.float32(-1e30)
    later = np.arange(P)[None, :] > np.arange(P)[:, None]
    freq = np.exp(-(np.arange(0, HD, 2, dtype=np.float32) / np.float32(HD)) * np.log(np.float32(10000.0)))
    angle = np.arange(T, dtype=np.float32)[None, :] * freq.astype(np.float32)[(np.arange(D) % HD) // 2][:, None]
    sign = np.where(np.arange(D) % 2 == 0, -1.0, 1.0)[:, None]
    cos = np.cos(angle.astype(np.float64)).astype(np.float32)
    sin = (np.sin(angle.astype(np.float64)) * sign).astype(np.float32)

    Wk, Wv = a["L0_attn_Wk"][:, spread], a["L0_attn_Wv"][:, spread]
    bk, bv = a["L0_attn_bk"][spread], a["L0_attn_bv"][spread]
    m = {
        "Wq": a["L0_attn_Wq"], "Wqs": a["L0_attn_Wq"][:, pair], "Wk": Wk, "Wks": Wk[:, pair], "Wv": Wv,
        "ident": np.eye(P, dtype=np.float32),
        "bq": cols(a["L0_attn_bq"]), "bqs": cols(a["L0_attn_bq"][pair]), "bk": cols(bk), "bks": cols(bk[pair]),
        "mask_ts": np.where(later, low, np.float32(0)), 
        "Wo": a["L0_attn_Wo"], "W1": a["L0_ffn_w1"], "W2": tiles(a["L0_ffn_w2"]),
        "Wq1": a["L1_attn_Wq"], "Wk1": a["L1_attn_Wk"], "Wv1": a["L1_attn_Wv"], "Wo1": a["L1_attn_Wo"],
        "A": a["L1_ffn_w1_w"].T, "B": a["L1_ffn_w2_w"].T, "H1": tiles(a["L1_ffn_h1_w"].T),
        "H2": tiles(a["L1_ffn_h2_w"].T), "W3": tiles(a["L1_ffn_w3_w"].T),
        "b1": cols(a["L0_ffn_b1"]), "sa": cols(a["L1_ffn_w1_s"]), "sb": cols(a["L1_ffn_w2_s"]),
        "s1": cols(a["L1_ffn_h1_s"]), "s2": cols(a["L1_ffn_h2_s"]),
    }
    pack = np.zeros((P, PACK_W), np.float32)
    for name, (at, width) in OFF.items():
        pack[:, at:at + width] = m[name]
    rows = np.concatenate([bv, a["L0_attn_bo"], a["L0_ffn_b2"], a["L1_attn_bo"], a["L1_ffn_w3_s"]])[None, :]
    arrays = {"x_in": a["L0_attn_x"], "xT_in": np.ascontiguousarray(a["L0_attn_x"][0].T), "pack": pack, "rows": rows,
              "cos": cos, "sin": sin}
    nc = bacc.Bacc("TRN2", target_bir_lowering=False, num_devices=1)
    args = [nc.dram_tensor(k, v.shape, mb.dt.from_np(v.dtype), kind="ExternalInput").ap() for k, v in arrays.items()]
    args.append(nc.dram_tensor("y_out", (1, T, D), mb.dt.float32, kind="ExternalOutput").ap())
    program(nc, *args)
    r = run_bass_kernel_spmd(nc, [arrays], core_ids=[0])
    return r.results[0]["y_out"]
```
